# Optimizing a Trainium2 kernel written in Bass

```python
import numpy as np
import jax
import jax.numpy as jnp

def _softmax(x, axis=-1):
    return jax.nn.softmax(x, axis=axis)

def _gelu(x):
    return jax.nn.gelu(x, approximate=True)

def _silu(x):
    return jax.nn.silu(x)

def _sigmoid(x):
    return jax.nn.sigmoid(x)

def _layernorm(x, axis=-1, eps=1e-05):
    m = jnp.mean(x, axis=axis, keepdims=True)
    v = jnp.var(x, axis=axis, keepdims=True)
    return (x - m) / jnp.sqrt(v + eps)

def _scatter_add(tgt, idx, src, axis=0):
    return tgt.at[idx].add(src)

def _segment_sum(src, seg, n):
    return jax.ops.segment_sum(src, seg, n)
kernel_name = 'mk_prb_d1_jaxref_r2_97a8f7'

def setup_inputs(seed: int=0):
    np.random.seed(seed)
    _w = jnp.asarray

    def _L0_attn_setup():
        import jax, jax.numpy as jnp
        import numpy as np
        from jax import lax
        B, S, D_IN = (4, 2048, 512)
        D_FAST, D_SLOW = (256, 256)
        Z_BIAS_FAST, Z_BIAS_SLOW = (2.0, -2.0)

        def _binop(q_i, q_j):
            a_i, b_i = q_i
            a_j, b_j = q_j
            return (a_i * a_j, a_j * b_i + b_j)

        def parallel_scan(a, b):
            _, h = lax.associative_scan(_binop, (a, b), axis=1)
            return h
        key = jax.random.key(seed)
        ks = jax.random.split(key, 6)
        scale = 0.02
        x = jax.random.normal(ks[0], (B, S, D_IN), dtype=jnp.float32)
        W_zf = jax.random.normal(ks[1], (D_IN, D_FAST), dtype=jnp.float32) * scale
        b_zf = jnp.full((D_FAST,), Z_BIAS_FAST, dtype=jnp.float32)
        W_hf = jax.random.normal(ks[2], (D_IN, D_FAST), dtype=jnp.float32) * scale
        b_hf = jnp.zeros((D_FAST,), dtype=jnp.float32)
        W_zs = jax.random.normal(ks[3], (D_IN, D_SLOW), dtype=jnp.float32) * scale
        b_zs = jnp.full((D_SLOW,), Z_BIAS_SLOW, dtype=jnp.float32)
        W_hs = jax.random.normal(ks[4], (D_IN, D_SLOW), dtype=jnp.float32) * scale
        b_hs = jnp.zeros((D_SLOW,), dtype=jnp.float32)
        W_g = jax.random.normal(ks[5], (D_FAST + D_SLOW, D_FAST + D_SLOW), dtype=jnp.float32) * scale
        b_g = jnp.zeros((D_FAST + D_SLOW,), dtype=jnp.float32)
        return {'x': x, 'W_zf': W_zf, 'b_zf': b_zf, 'W_hf': W_hf, 'b_hf': b_hf, 'W_zs': W_zs, 'b_zs': b_zs, 'W_hs': W_hs, 'b_hs': b_hs, 'W_g': W_g, 'b_g': b_g}
    _L0_attn_in = _L0_attn_setup()

    def _L0_ffn_setup():
        import jax, jax.numpy as jnp
        import numpy as np
        D_MODEL = 512
        EXPERT_DIM = 256
        N_EXPERTS = 8
        TOP_K = 2

        def _sq_relu(h):
            return jnp.square(jax.nn.relu(h))
        key = jax.random.key(seed)
        ks = jax.random.split(key, 6)
        s = 0.02
        x = jax.random.normal(ks[0], (2, 1024, D_MODEL), dtype=jnp.float32)
        Ws1 = jax.random.normal(ks[1], (D_MODEL, EXPERT_DIM), dtype=jnp.float32) * s
        Ws2 = jax.random.normal(ks[2], (EXPERT_DIM, D_MODEL), dtype=jnp.float32) * s
        W1 = jax.random.normal(ks[3], (N_EXPERTS, D_MODEL, EXPERT_DIM), dtype=jnp.float32) * s
        W2 = jax.random.normal(ks[4], (N_EXPERTS, EXPERT_DIM, D_MODEL), dtype=jnp.float32) * s
        Wr = jax.random.normal(ks[5], (D_MODEL, N_EXPERTS), dtype=jnp.float32) * s
        return {'x': x, 'Ws1': Ws1, 'Ws2': Ws2, 'W1': W1, 'W2': W2, 'Wr': Wr}
    _L0_ffn_in = _L0_ffn_setup()
    _d = {'L0_attn_x': _L0_attn_in['x'], 'L0_attn_W_zf': _L0_attn_in['W_zf'], 'L0_attn_b_zf': _L0_attn_in['b_zf'], 'L0_attn_W_hf': _L0_attn_in['W_hf'], 'L0_attn_b_hf': _L0_attn_in['b_hf'], 'L0_attn_W_zs': _L0_attn_in['W_zs'], 'L0_attn_b_zs': _L0_attn_in['b_zs'], 'L0_attn_W_hs': _L0_attn_in['W_hs'], 'L0_attn_b_hs': _L0_attn_in['b_hs'], 'L0_attn_W_g': _L0_attn_in['W_g'], 'L0_attn_b_g': _L0_attn_in['b_g'], 'L0_ffn_Ws1': _L0_ffn_in['Ws1'], 'L0_ffn_Ws2': _L0_ffn_in['Ws2'], 'L0_ffn_W1': _L0_ffn_in['W1'], 'L0_ffn_W2': _L0_ffn_in['W2'], 'L0_ffn_Wr': _L0_ffn_in['Wr']}
    _x0 = _d['L0_attn_x']
    _d['L0_attn_x'] = jax.random.normal(jax.random.fold_in(jax.random.key(seed), 1), (1, 8192, 512), dtype=_x0.dtype)
    del _x0
    return _d

def reference(L0_attn_x, L0_attn_W_zf, L0_attn_b_zf, L0_attn_W_hf, L0_attn_b_hf, L0_attn_W_zs, L0_attn_b_zs, L0_attn_W_hs, L0_attn_b_hs, L0_attn_W_g, L0_attn_b_g, L0_ffn_Ws1, L0_ffn_Ws2, L0_ffn_W1, L0_ffn_W2, L0_ffn_Wr):

    def _L0_attn_ref(x, W_zf, b_zf, W_hf, b_hf, W_zs, b_zs, W_hs, b_hs, W_g, b_g):
        import jax, jax.numpy as jnp
        import numpy as np
        from jax import lax
        B, S, D_IN = (4, 2048, 512)
        D_FAST, D_SLOW = (256, 256)
        Z_BIAS_FAST, Z_BIAS_SLOW = (2.0, -2.0)

        def _binop(q_i, q_j):
            a_i, b_i = q_i
            a_j, b_j = q_j
            return (a_i * a_j, a_j * b_i + b_j)

        def parallel_scan(a, b):
            _, h = lax.associative_scan(_binop, (a, b), axis=1)
            return h
        z_fast = jax.nn.sigmoid(jnp.einsum('bsd,df->bsf', x, W_zf) + b_zf)
        h_tilde_fast = jnp.einsum('bsd,df->bsf', x, W_hf) + b_hf
        h_fast = parallel_scan(1.0 - z_fast, z_fast * h_tilde_fast)
        z_slow = jax.nn.sigmoid(jnp.einsum('bsd,df->bsf', x, W_zs) + b_zs)
        h_tilde_slow = jnp.einsum('bsd,df->bsf', x, W_hs) + b_hs
        h_slow = parallel_scan(1.0 - z_slow, z_slow * h_tilde_slow)
        h_combined = jnp.concatenate([h_fast, h_slow], axis=-1)
        gate = jax.nn.sigmoid(jnp.einsum('bsc,cd->bsd', h_combined, W_g) + b_g)
        return gate * h_combined

    def _L0_ffn_ref(x, Ws1, Ws2, W1, W2, Wr):
        import jax, jax.numpy as jnp
        import numpy as np
        D_MODEL = 512
        EXPERT_DIM = 256
        N_EXPERTS = 8
        TOP_K = 2

        def _sq_relu(h):
            return jnp.square(jax.nn.relu(h))
        shape = x.shape
        xf = x.reshape(-1, D_MODEL)
        out_shared = _sq_relu(xf @ Ws1) @ Ws2
        logits = xf @ Wr
        top_vals, top_idx = jax.lax.top_k(logits, TOP_K)
        rw = jax.nn.softmax(top_vals.astype(jnp.float32), axis=-1).astype(x.dtype)
        onehot = jax.nn.one_hot(top_idx, N_EXPERTS, dtype=x.dtype)
        prob = jnp.einsum('tk,tke->te', rw, onehot)
        prob = jnp.trunc(prob)
        h = _sq_relu(jnp.einsum('td,edf->tef', xf, W1))
        y = jnp.einsum('tef,efd->ted', h, W2)
        out_routed = jnp.einsum('ted,te->td', y, prob)
        return (out_shared + out_routed).reshape(shape)
    x = L0_attn_x
    xn = _layernorm(x, axis=-1)
    x = x + _L0_attn_ref(xn, L0_attn_W_zf, L0_attn_b_zf, L0_attn_W_hf, L0_attn_b_hf, L0_attn_W_zs, L0_attn_b_zs, L0_attn_W_hs, L0_attn_b_hs, L0_attn_W_g, L0_attn_b_g) + _L0_ffn_ref(xn, L0_ffn_Ws1, L0_ffn_Ws2, L0_ffn_W1, L0_ffn_W2, L0_ffn_Wr)
    return x

_drawn_inputs = setup_inputs


def setup_inputs(seed=0):
    import zlib

    import numpy as np

    out = dict(_drawn_inputs(seed))
    spreads = {'L0_attn_b_zf': (2.0, 0.6),
     'L0_attn_b_hf': (0.0, 0.1),
     'L0_attn_b_zs': (-2.0, 0.6),
     'L0_attn_b_hs': (0.0, 0.1),
     'L0_attn_b_g': (0.0, 0.8)}
    factors = {'L0_attn_W_zf': 5.285, 'L0_attn_W_zs': 3.289, 'L0_attn_W_g': 5.195}
    for name, (base, spread) in spreads.items():
        noise = np.random.default_rng([zlib.crc32(name.encode()), seed]).standard_normal(out[name].shape)
        drawn = base * np.exp(spread * noise) if base else spread * noise
        out[name] = jnp.asarray(drawn.astype(out[name].dtype))
    for name, factor in factors.items():
        out[name] = (out[name] * factor).astype(out[name].dtype)
    return out
```

```python
from contextlib import ExitStack

import concourse.bass as bass
from concourse import mybir

F32 = mybir.dt.float32
F32R = mybir.dt.float32r
I32 = mybir.dt.int32
ALU = mybir.AluOpType
ACT = mybir.ActivationFunctionType
AX_X = mybir.AxisListType.X

P = 128
TOK = 512
SB = TOK // P
EPS = 1e-5


def minlstm_gated_moe_kernel(
    nc, x, w_zf, b_zf, w_hf, b_hf, w_zs, b_zs, w_hs, b_hs, w_g, b_g, w_s1, w_s2, w_e1, w_e2, w_r, out
):
    _, S, D = x.shape
    DF = w_zf.shape[1]
    F = w_s1.shape[1]
    NE = w_r.shape[1]
    NT = S // TOK
    NB = S // P
    K = D // P
    KF = F // P
    CF = DF // P
    assert 2 * DF == D and K == 4 and SB == 4 and KF == 2 and NT % 2 == 0 and S % TOK == 0
    NPJ, NTP = 5, 3
    TP = K + KF
    PU = 4 * K

    x_v = x.rearrange("a (b p) d -> p (a b) d", p=P)
    out_v = out.rearrange("a (b p) d -> p (a b) d", p=P)

    ctx = ExitStack()
    with ctx:
        def sb(name, shape, dt=F32):
            return ctx.enter_context(nc.sbuf_tensor(name, shape, dt))

        def sem(name):
            return ctx.enter_context(nc.semaphore(name))

        wz_hi, wz_lo = sb("wz_hi", [P, K, D], F32R), sb("wz_lo", [P, K, D], F32R)
        wh_hi, wh_lo = sb("wh_hi", [P, K, D], F32R), sb("wh_lo", [P, K, D], F32R)
        wg_hi, wg_lo = sb("wg_hi", [P, K, D], F32R), sb("wg_lo", [P, K, D], F32R)
        w1_hi, w1_lo = sb("w1_hi", [P, K, F + NE], F32R), sb("w1_lo", [P, K, F + NE], F32R)
        w2_hi, w2_lo = sb("w2_hi", [P, KF, D], F32R), sb("w2_lo", [P, KF, D], F32R)
        wz_in, wh_in = sb("wz_in", [P, K, D]), sb("wh_in", [P, K, D])
        w1_in = sb("w1_in", [P, K, F + NE])

        x_tok = sb("x_tok", [P, 2, SB, D])
        xn = sb("xn", [P, SB, D])
        stats = sb("stats", [P, SB, 6])
        mean_var = sb("mean_var", [P, SB, 2])
        var_eps = sb("var_eps", [P, SB])
        minus_half = sb("minus_half", [P, SB])
        rstd = sb("rstd", [P, SB])
        mean_all, rstd_all = sb("mean_all", [P, NB]), sb("rstd_all", [P, NB])
        xT_hi, xT_lo = sb("xT_hi", [P, K, TOK], F32R), sb("xT_lo", [P, K, TOK], F32R)
        z = sb("z", [P, 2, TOK])
        a = sb("a", [P, 2, TOK])
        zh = sb("zh", [P, 2, TOK])
        h = sb("h", [P, K, TOK])
        h_hi, h_lo = sb("h_hi", [P, K, TOK], F32R), sb("h_lo", [P, K, TOK], F32R)
        gate = sb("gate", [P, K, TOK])
        relu = sb("relu", [P, 2, F])
        hid = sb("hid", [P, SB, F])
        hidT_hi, hidT_lo = sb("hidT_hi", [P, KF, TOK], F32R), sb("hidT_lo", [P, KF, TOK], F32R)
        y = sb("y", [P, SB, D])
        wg_in = gate
        w2_in = y[:, 0:KF, :]

        bias_rows = sb("bias_rows", [3 * K, P])
        bias = sb("bias", [P, 3 * K])
        neg_bz = sb("neg_bz", [P, K])
        ident = sb("ident", [P, P])
        ones = sb("ones", [P, 1])
        logits = sb("logits", [P, NB, NE])
        top8 = sb("top8", [P, SB, 8])
        top2 = sb("top2", [P, NB, 2])
        gap = sb("gap", [P, NB])
        expo = sb("expo", [P, NB])
        denom = sb("denom", [P, NB])
        is_one = sb("is_one", [P, NB])
        n_ones = sb("n_ones", [P, 1])
        flag = sb("flag", [1, 1], I32)
        prob = sb("prob", [P, NB, NE])

        pj = [ctx.enter_context(nc.psum_tensor(f"pj{i}", [P, TOK], F32)) for i in range(NPJ)]
        tp = [ctx.enter_context(nc.psum_tensor(f"tp{i}", [P, TOK], F32)) for i in range(NTP)]

        x0_loaded = [sem(f"x0_loaded{s}") for s in range(SB)]
        x_loaded = sem("x_loaded")
        bias_loaded = sem("bias_loaded")
        W = ["zf", "hf", "zs", "hs", "w1", "g", "w2"]
        w_loaded = {n: sem(f"w_loaded_{n}") for n in W}
        w_hi_ready, w_lo_ready = sem("w_hi_ready"), sem("w_lo_ready")
        ident_zeroed, ident_ready, const_ready = sem("ident_zeroed"), sem("ident_ready"), sem("const_ready")
        bias_turned, bias_ready = sem("bias_turned"), sem("bias_ready")
        stats_ready, mean_var_ready, var_eps_ready = sem("stats_ready"), sem("mean_var_ready"), sem("var_eps_ready")
        rstd_ready, xn_ready, ln_kept = sem("rstd_ready"), sem("xn_ready"), sem("ln_kept")
        turned, turned_hi, turned_lo = sem("turned"), sem("turned_hi"), sem("turned_lo")
        products_done = sem("products_done")
        z_a_ready, zh_ready, scan_done = sem("z_a_ready"), sem("zh_ready"), sem("scan_done")
        h_hi_ready, h_lo_ready = sem("h_hi_ready"), sem("h_lo_ready")
        relu_ready, top8_ready, hid_ready = sem("relu_ready"), sem("top8_ready"), sem("hid_ready")
        top2_kept = sem("top2_kept")
        gate_ready, gated_ready = sem("gate_ready"), sem("gated_ready")
        sums_done, y_ready, y_stored = sem("sums_done"), sem("y_ready"), sem("y_stored")
        gap_ready, expo_ready, route_step = sem("gap_ready"), sem("expo_ready"), sem("route_step")
        counted, flag_ready = sem("counted"), sem("flag_ready")

        def x_chunk(t, k):
            return TP * t + k

        def hid_chunk(t, f):
            return TP * t + K + f

        def tp_bank(n_in_tile):
            return tp[(n_in_tile + 2) % NTP]

        Z_H, FFN1, GATE, OUT = 0, 2 * K, 2 * K + SB, 2 * K + SB + K

        def pj_bank(u):
            return pj[u % NPJ]

        def reached(eng, semaphore, value):
            if not (isinstance(value, int) and value <= 0):
                eng.wait_ge(semaphore, value)

        def tiles(eng, one_tile):
            one_tile(0, 0)
            with eng.Fori(0, NT // 2 - 1) as i:
                one_tile(2 * i + 1, 1)
                one_tile(2 * i + 2, 0)
            one_tile(NT - 1, 1, last=True)

        fb_loaded, fb_xn_ready, fb_turned, fb_xT_ready = (
            sem(n) for n in ("fb_loaded", "fb_xn_ready", "fb_turned", "fb_xT_ready"))
        fb_w_loaded, fb_hid_done, fb_relu, fb_hid_ready = (
            sem(n) for n in ("fb_w_loaded", "fb_hid_done", "fb_relu", "fb_hid_ready"))
        fb_hid_turned, fb_hidT_ready, fb_y_done, fb_y_added = (
            sem(n) for n in ("fb_hid_turned", "fb_hidT_ready", "fb_y_done", "fb_y_added"))
        fb_route = sem("fb_route")
        fb_w1, fb_w2 = wz_in[:, :, 0:F], wh_in[:, 0:KF, :]
        fb_xT, fb_hidT = h, zh

        block = ctx.enter_context(nc.Block())

        @block.sync
        def _(sp):
            for s in range(SB):
                sp.dma_start(x_tok[:, 0, s, :], x_v[:, s, :]).then_inc(x0_loaded[s], 16)
            sp.dma_start(wz_in[:, :, DF:D], w_zs.rearrange("(k p) f -> p k f", p=P)).then_inc(w_loaded["zs"], 16)
            sp.dma_start(wh_in[:, :, DF:D], w_hs.rearrange("(k p) f -> p k f", p=P)).then_inc(w_loaded["hs"], 16)
            sp.dma_start(x_tok[:, 1, :, :], x_v[:, SB:2 * SB, :]).then_inc(x_loaded, 16)
            sp.dma_start(wg_in[:, :, :], w_g.rearrange("(k p) f -> p k f", p=P)).then_inc(w_loaded["g"], 16)

            def store(t):
                sp.wait_ge(y_ready, SB * t + SB)
                sp.dma_start(out_v[:, bass.ts(t, SB), :], y[:, :, :]).then_inc(y_stored, 16)

            with sp.Fori(0, NT // 2 - 1) as i:
                for parity in range(2):
                    store(2 * i + parity)
                    sp.dma_start(x_tok[:, parity, :, :], x_v[:, bass.ts(2 * i + parity + 2, SB), :]).then_inc(x_loaded, 16)
            store(NT - 2)
            for s in range(SB):
                sp.wait_ge(y_ready, SB * (NT - 1) + s + 1)
                sp.dma_start(out_v[:, SB * (NT - 1) + s, :], y[:, s, :]).then_inc(y_stored, 16)
            sp.wait_ge(y_stored, 16 * (NT - 1 + SB))

            sp.wait_ge(flag_ready, 1)
            routed = sp.value_load(flag[0:1, 0:1])
            with sp.If(routed > 0):
                with sp.Fori(0, NT) as t:
                    sp.wait_ge(y_stored, t * 16 + 16 * (NT - 1 + SB))
                    sp.dma_start(x_tok[:, 0, :, :], x_v[:, bass.ts(t, SB), :]).then_inc(fb_loaded, 16)
                    sp.dma_start(y[:, :, :], out_v[:, bass.ts(t, SB), :]).then_inc(fb_loaded, 16)
                    with sp.Fori(0, NE) as e:
                        sp.wait_ge(fb_y_done, (t * NE + e) * SB + 1)
                        sp.dma_start(fb_w1, w_e1[bass.ds(e, 1), :, :].rearrange("a (k p) f -> p (a k) f", p=P)).then_inc(fb_w_loaded, 16)
                        sp.dma_start(fb_w2, w_e2[bass.ds(e, 1), :, :].rearrange("a (k p) f -> p (a k) f", p=P)).then_inc(fb_w_loaded, 16)
                    sp.wait_ge(fb_y_added, (t + 1) * (NE * SB) + 1)
                    sp.dma_start(out_v[:, bass.ts(t, SB), :], y[:, :, :]).then_inc(y_stored, 16)
                sp.wait_ge(y_stored, 16 * (2 * NT - 1 + SB))

        @block.gpsimd
        def _(pool):
            pool.memset(ident[:, :], 0.0).then_inc(ident_zeroed, 1)
            pool.memset(minus_half[:, :], -0.5).then_inc(const_ready, 1)
            pool.memset(ones[:, :], 1.0).then_inc(const_ready, 1)
            pool.wait_ge(ident_zeroed, 1)
            pool.affine_select(out=ident[:, :], in_=ident[:, :], compare_op=ALU.not_equal, fill=1.0,
                               base=0, pattern=[[-1, P]], channel_multiplier=1).then_inc(ident_ready, 1)
            pool.dma_start(w1_in[:, :, 0:F], w_s1.rearrange("(k p) f -> p k f", p=P)).then_inc(w_loaded["w1"], 16)
            pool.dma_start(w1_in[:, :, F:F + NE], w_r.rearrange("(k p) f -> p k f", p=P)).then_inc(w_loaded["w1"], 16)
            pool.dma_start(w2_in, w_s2.rearrange("(k p) f -> p k f", p=P)).then_inc(w_loaded["w2"], 16)

            def inverse_std(t):
                pool.wait_ge(var_eps_ready, t + 1)
                if isinstance(t, int) and t == 0:
                    pool.wait_ge(const_ready, 2)
                pool.tensor_tensor(rstd[:, :], var_eps[:, :], minus_half[:, :], ALU.pow).then_inc(rstd_ready, 1)

            def split_lo(n, lo, full, hi):
                pool.wait_ge(w_hi_ready, W.index(n) + 1)
                pool.tensor_tensor(lo, full, hi.bitcast(F32), ALU.subtract).then_inc(w_lo_ready, 1)

            split_lo("zf", wz_lo[:, :, 0:DF], wz_in[:, :, 0:DF], wz_hi[:, :, 0:DF])
            inverse_std(0)
            split_lo("hf", wh_lo[:, :, 0:DF], wh_in[:, :, 0:DF], wh_hi[:, :, 0:DF])
            split_lo("zs", wz_lo[:, :, DF:D], wz_in[:, :, DF:D], wz_hi[:, :, DF:D])
            split_lo("hs", wh_lo[:, :, DF:D], wh_in[:, :, DF:D], wh_hi[:, :, DF:D])
            inverse_std(1)
            split_lo("w1", w1_lo[:, :, :], w1_in[:, :, :], w1_hi[:, :, :])
            split_lo("g", wg_lo[:, :, :], wg_in[:, :, :], wg_hi[:, :, :])
            split_lo("w2", w2_lo[:, :, :], w2_in, w2_hi[:, :, :])
            with pool.Fori(2, NT) as t:
                pool.wait_ge(ln_kept, t * 2)
                inverse_std(t)

        @block.scalar
        def _(act):
            act.dma_start(wz_in[:, :, 0:DF], w_zf.rearrange("(k p) f -> p k f", p=P)).then_inc(w_loaded["zf"], 16)
            act.dma_start(wh_in[:, :, 0:DF], w_hf.rearrange("(k p) f -> p k f", p=P)).then_inc(w_loaded["hf"], 16)
            rows = 0
            for b in (b_zf, b_zs, b_hf, b_hs, b_g):
                n = b.shape[0] // P
                act.dma_start(bias_rows[rows:rows + n, :], b.rearrange("(c p) -> c p", p=P)).then_inc(bias_loaded, 16)
                rows += n

            def split_hi(n, hi, full, loads=1):
                act.wait_ge(w_loaded[n], 16 * loads)
                act.activation(hi, full, ACT.Copy).then_inc(w_hi_ready, 1)

            def turned_hi_part(number, bank, dst):
                act.wait_ge(turned, number + 1)
                act.activation(dst, bank[:, :], ACT.Copy).then_inc(turned_hi, 1)

            split_hi("zf", wz_hi[:, :, 0:DF], wz_in[:, :, 0:DF])
            split_hi("hf", wh_hi[:, :, 0:DF], wh_in[:, :, 0:DF])
            for k in range(K):
                turned_hi_part(x_chunk(0, k), tp_bank(k), xT_hi[:, k, :])
            split_hi("zs", wz_hi[:, :, DF:D], wz_in[:, :, DF:D])
            split_hi("hs", wh_hi[:, :, DF:D], wh_in[:, :, DF:D])

            def one_tile(t, parity, last=False):
                for c in range(K):
                    act.wait_ge(products_done, PU * t + 2 * c + 1)
                    reached(act, scan_done, K * t + c - 1)
                    if isinstance(t, int) and t == 0 and c == 0:
                        act.wait_ge(bias_ready, 2)
                    u = pj_bank(Z_H + 2 * c)
                    act.activation(z[:, c % 2, :], u[:, :], ACT.Sigmoid, bias=bias[:, c:c + 1]).then_inc(z_a_ready, 1)
                    act.activation(a[:, c % 2, :], u[:, :], ACT.Sigmoid, bias=neg_bz[:, c:c + 1], scale=-1.0).then_inc(z_a_ready, 1)
                    if c:
                        hi_part(t, c - 1)
                    if isinstance(t, int) and t == 0 and c == 0:
                        split_hi("w1", w1_hi[:, :, :], w1_in[:, :, :], loads=2)
                    if isinstance(t, int) and t == 0 and c == 1:
                        split_hi("g", wg_hi[:, :, :], wg_in[:, :, :])
                    if isinstance(t, int) and t == 0 and c == 2:
                        split_hi("w2", w2_hi[:, :, :], w2_in)
                for s in range(SB):
                    act.wait_ge(products_done, PU * t + FFN1 + s + 1)
                    reached(act, hid_ready, SB * t + s - 1)
                    act.activation(relu[:, s % 2, :], pj_bank(FFN1 + s)[:, 0:F], ACT.Relu).then_inc(relu_ready, 1)
                    if s == 1:
                        hi_part(t, K - 1)
                order = [(hid_chunk(t, f), tp_bank(K + f), hidT_hi[:, f, :]) for f in range(KF)]
                if not last:
                    order += [(x_chunk(t + 1, k), tp_bank(k), xT_hi[:, k, :]) for k in range(K)]
                for m in range(K):
                    act.wait_ge(products_done, PU * t + GATE - 0 + m + 1)
                    act.activation(gate[:, m, :], pj_bank(GATE + m)[:, :], ACT.Sigmoid,
                                   bias=bias[:, 2 * K + m:2 * K + m + 1]).then_inc(gate_ready, 1)
                    if m < len(order):
                        turned_hi_part(*order[m])
                for chunk in order[K:]:
                    turned_hi_part(*chunk)

            def hi_part(t, c):
                act.wait_ge(scan_done, K * t + c + 1)
                act.activation(h_hi[:, c, :], h[:, c, :], ACT.Copy).then_inc(h_hi_ready, 1)

            tiles(act, one_tile)
            act.wait_ge(gap_ready, 1)
            act.activation(expo[:, :], gap[:, :], ACT.Exp).then_inc(expo_ready, 1)

        @block.vector
        def _(dve):
            def ln_stats(t, parity):
                reached(dve, mean_var_ready, SB * t)
                if not isinstance(t, int) or t:
                    dve.wait_ge(x_loaded, 16 * t)
                for s in range(SB):
                    if isinstance(t, int) and t == 0:
                        dve.wait_ge(x0_loaded[s], 16)
                    dve.bn_stats(stats[:, s, :], x_tok[:, parity, s, :]).then_inc(stats_ready, 1)

            def ln_stats_done(t):
                dve.wait_ge(stats_ready, SB * t + SB)
                reached(dve, ln_kept, 2 * t)

            def ln_mean_var(t):
                for s in range(SB):
                    dve.bn_aggr(mean_var[:, s, :], stats[:, s, :]).then_inc(mean_var_ready, 1)
                dve.wait_ge(mean_var_ready, SB * t + SB)
                reached(dve, rstd_ready, t)
                dve.tensor_scalar(var_eps[:, :], mean_var[:, :, 1], EPS, None, ALU.add).then_inc(var_eps_ready, 1)

            def ln_apply(t, parity, blocks):
                for s in blocks:
                    dve.wait_ge(rstd_ready, t + 1)
                    reached(dve, turned, TP * (t - 1) + K)
                    dve.tensor_scalar(xn[:, s, :], x_tok[:, parity, s, :], mean_var[:, s, 0:1],
                                      rstd[:, s:s + 1], ALU.subtract, ALU.mult).then_inc(xn_ready, 1)
                if blocks[-1] == SB - 1:
                    dve.tensor_copy(mean_all[:, bass.ts(t, SB)], mean_var[:, :, 0]).then_inc(ln_kept, 1)
                    dve.tensor_copy(rstd_all[:, bass.ts(t, SB)], rstd[:, :]).then_inc(ln_kept, 1)

            def turned_lo_part(number, bank, hi, lo):
                dve.wait_ge(turned_hi, number + 1)
                dve.tensor_tensor(lo, bank[:, :], hi.bitcast(F32), ALU.subtract).then_inc(turned_lo, 1)

            def lo_part(t, c):
                dve.wait_ge(h_hi_ready, K * t + c + 1)
                dve.tensor_tensor(h_lo[:, c, :], h[:, c, :], h_hi[:, c, :].bitcast(F32),
                                  ALU.subtract).then_inc(h_lo_ready, 1)

            def one_tile(t, parity, last=False):
                first = isinstance(t, int) and t == 0
                for c in range(K):
                    dve.wait_ge(z_a_ready, 2 * (K * t + c) + 1)
                    dve.wait_ge(products_done, PU * t + 2 * c + 2)
                    reached(dve, scan_done, K * t + c - 1)
                    dve.scalar_tensor_tensor(zh[:, c % 2, :], pj_bank(Z_H + 2 * c + 1)[:, :], bias[:, K + c:K + c + 1],
                                             z[:, c % 2, :], ALU.add, ALU.mult).then_inc(zh_ready, 1)
                    if c:
                        lo_part(t, c - 1)
                    elif not last:
                        ln_stats(t + 1, 1 - parity)
                    dve.wait_ge(z_a_ready, 2 * (K * t + c) + 2)
                    dve.wait_ge(zh_ready, K * t + c + 1)
                    reached(dve, gated_ready, K * t)
                    if c == 0 and not last:
                        ln_stats_done(t + 1)
                    dve.tensor_tensor_scan(h[:, c, :], a[:, c % 2, :], zh[:, c % 2, :],
                                           0.0 if first else h[:, c, TOK - 1:TOK],
                                           ALU.mult, ALU.add).then_inc(scan_done, 1)
                    if not last:
                        if c == 0:
                            ln_mean_var(t + 1)
                        elif c < 3:
                            ln_apply(t + 1, 1 - parity, (2 * c - 2, 2 * c - 1))
                for s in range(SB):
                    bank = pj_bank(FFN1 + s)
                    dve.wait_ge(relu_ready, SB * t + s + 1)
                    if s == 0:
                        reached(dve, top2_kept, t)
                    dve.tensor_copy(logits[:, bass.ds(t * SB + s, 1), :], bank[:, F:F + NE].rearrange("p (a e) -> p a e", a=1))
                    dve.max(top8[:, s, :], bank[:, F:F + NE]).then_inc(top8_ready, 1)
                    dve.tensor_tensor(hid[:, s, :], bank[:, 0:F], relu[:, s % 2, :], ALU.mult).then_inc(hid_ready, 1)
                    if s == 1:
                        lo_part(t, K - 1)
                dve.wait_ge(top8_ready, SB * t + SB)
                dve.tensor_copy(top2[:, bass.ts(t, SB), :], top8[:, :, 0:2]).then_inc(top2_kept, 1)
                if last:
                    dve.wait_ge(top2_kept, NT)
                    dve.tensor_tensor(gap[:, :], top2[:, :, 1], top2[:, :, 0], ALU.subtract).then_inc(gap_ready, 1)
                order = [(hid_chunk(t, f), tp_bank(K + f), hidT_hi[:, f, :], hidT_lo[:, f, :]) for f in range(KF)]
                if not last:
                    order += [(x_chunk(t + 1, k), tp_bank(k), xT_hi[:, k, :], xT_lo[:, k, :]) for k in range(K)]
                for m in range(K):
                    dve.wait_ge(gate_ready, K * t + m + 1)
                    dve.tensor_tensor(gate[:, m, :], gate[:, m, :], h[:, m, :], ALU.mult).then_inc(gated_ready, 1)
                    if m < len(order):
                        turned_lo_part(*order[m])
                for chunk in order[K:]:
                    turned_lo_part(*chunk)
                reached(dve, y_stored, 16 * t)
                for s in range(SB):
                    dve.wait_ge(sums_done, SB * t + s + 1)
                    dve.tensor_tensor(y[:, s, :], pj_bank(OUT + s)[:, :], x_tok[:, parity, s, :], ALU.add).then_inc(y_ready, 1)

            ln_stats(0, 0)
            ln_stats_done(0)
            ln_mean_var(0)
            ln_apply(0, 0, range(SB))
            dve.wait_ge(bias_turned, 1)
            dve.tensor_copy(bias[:, :], pj[NPJ - 1][:, 0:3 * K]).then_inc(bias_ready, 1)
            dve.tensor_scalar(neg_bz[:, :], pj[NPJ - 1][:, 0:K], -1.0, None, ALU.mult).then_inc(bias_ready, 1)
            for k in range(K):
                turned_lo_part(x_chunk(0, k), tp_bank(k), xT_hi[:, k, :], xT_lo[:, k, :])
            tiles(dve, one_tile)

            dve.wait_ge(expo_ready, 1)
            dve.tensor_scalar(denom[:, :], expo[:, :], 1.0, None, ALU.add).then_inc(route_step, 1)
            dve.wait_ge(route_step, 1)
            dve.tensor_scalar(is_one[:, :], denom[:, :], 1.0, None, ALU.is_le).then_inc(route_step, 1)
            dve.wait_ge(route_step, 2)
            dve.tensor_reduce(n_ones[:, :], is_one[:, :], AX_X, ALU.add).then_inc(route_step, 1)
            dve.wait_ge(counted, 1)
            dve.tensor_copy(flag[:, :], tp[0][0:1, 0:1]).then_inc(flag_ready, 1)

            dve.wait_ge(flag_ready, 1)
            routed = dve.value_load(flag[0:1, 0:1])
            with dve.If(routed > 0):
                top1 = top2[:, :, 0:1].to_broadcast([P, NB, NE])
                dve.tensor_tensor(prob[:, :, :], logits[:, :, :], top1, ALU.is_equal).then_inc(fb_route, 1)
                dve.wait_ge(fb_route, 1)
                ones_b = is_one[:, :].rearrange("p (b a) -> p b a", a=1).to_broadcast([P, NB, NE])
                dve.tensor_tensor(prob[:, :, :], prob[:, :, :], ones_b, ALU.mult).then_inc(fb_route, 1)
                dve.wait_ge(fb_route, 2)
                prob_flat = prob[:, :, :].rearrange("p b e -> p (b e)")
                dve.sem_inc(fb_y_added, 1)
                with dve.Fori(0, NT) as t:
                    dve.wait_ge(fb_loaded, (t + 1) * 32)
                    for s in range(SB):
                        dve.tensor_scalar(xn[:, s, :], x_tok[:, 0, s, :], mean_all[:, bass.ds(t * SB + s, 1)],
                                          rstd_all[:, bass.ds(t * SB + s, 1)],
                                          ALU.subtract, ALU.mult).then_inc(fb_xn_ready, 1)
                    for k in range(K):
                        dve.wait_ge(fb_turned, t * K + k + 1)
                        dve.tensor_copy(fb_xT[:, k, :], pj[k][:, :]).then_inc(fb_xT_ready, 1)
                    with dve.Fori(0, NE) as e:
                        for s in range(SB):
                            dve.wait_ge(fb_hid_done, (t * NE + e) * SB + s + 1)
                            dve.tensor_scalar(relu[:, 0, :], pj[s][:, 0:F], 0.0, None, ALU.max).then_inc(fb_relu, 1)
                            dve.wait_ge(fb_relu, (t * NE + e) * SB + s + 1)
                            dve.scalar_tensor_tensor(hid[:, s, :], pj[s][:, 0:F],
                                                     prob_flat[:, bass.ds(t * (SB * NE) + s * NE + e, 1)],
                                                     relu[:, 0, :], ALU.mult, ALU.mult).then_inc(fb_hid_ready, 1)
                            dve.wait_ge(fb_hid_ready, (t * NE + e) * SB + s + 1)
                        for f in range(KF):
                            dve.wait_ge(fb_hid_turned, (t * NE + e) * KF + f + 1)
                            dve.tensor_copy(fb_hidT[:, f, :], tp[f][:, :]).then_inc(fb_hidT_ready, 1)
                        for s in range(SB):
                            dve.wait_ge(fb_y_done, (t * NE + e) * SB + s + 2)
                            dve.tensor_tensor(y[:, s, :], pj[s][:, :], y[:, s, :], ALU.add).then_inc(fb_y_added, 1)
                        dve.wait_ge(fb_y_added, (t * NE + e + 1) * SB + 1)

        @block.tensor
        def _(pe):
            def three(dst, pairs, hook=None):
                for i, (s_hi, s_lo, m_hi, m_lo) in enumerate(pairs):
                    if hook:
                        hook(i)
                    for j, (st, mv) in enumerate(((s_hi, m_hi), (s_lo, m_hi), (s_hi, m_lo))):
                        end = i == len(pairs) - 1 and j == 2
                        mm = pe.matmul(dst, st, mv, start=(i == 0 and j == 0), stop=end)
                return mm

            def turn(bank, sources):
                for s, src in enumerate(sources):
                    mm = pe.transpose(bank[:, s * P:(s + 1) * P], src, ident[:, :])
                mm.then_inc(turned, 1)

            def turn_x(t, k):
                if k == 0:
                    pe.wait_ge(xn_ready, SB * t + SB)
                reached(pe, turned_lo, x_chunk(t, k) - NTP + 1)
                turn(tp_bank(k), [xn[:, s, k * P:(k + 1) * P] for s in range(SB)])

            def turn_hid(t, f):
                if f == 0:
                    pe.wait_ge(hid_ready, SB * t + SB)
                reached(pe, turned_lo, hid_chunk(t, f) - NTP + 1)
                turn(tp_bank(K + f), [hid[:, s, f * P:(f + 1) * P] for s in range(SB)])

            def one_tile(t, parity, last=False):
                first = isinstance(t, int) and t == 0

                for c in range(K):
                    for kind, (w_hi, w_lo) in enumerate(((wz_hi, wz_lo), (wh_hi, wh_lo))):
                        u = 2 * c + kind
                        if u == 0:
                            reached(pe, gate_ready, K * t)
                        elif u < NPJ:
                            reached(pe, y_ready, SB * t - SB + u)
                        elif u % 2 == 1:
                            pe.wait_ge(z_a_ready, 2 * (K * t + (u - NPJ) // 2) + 2)
                        else:
                            pe.wait_ge(zh_ready, K * t + (u - NPJ) // 2 + 1)
                        if first:
                            pe.wait_ge(w_lo_ready, (1, 2, 3, 4)[kind + 2 * (c // CF)])
                            if u == NPJ - 1:
                                pe.wait_ge(bias_ready, 2)
                        col = slice(c * P, (c + 1) * P)
                        three(pj_bank(u)[:, :],
                              [(w_hi[:, k, col], w_lo[:, k, col], xT_hi[:, k, :], xT_lo[:, k, :]) for k in range(K)],
                              (lambda k: pe.wait_ge(turned_lo, x_chunk(t, k) + 1)) if u == 0 else None,
                              ).then_inc(products_done, 1)
                for s in range(SB):
                    if s % 2:
                        pe.wait_ge(z_a_ready, 2 * (K * t + (3 + s) // 2) + 2)
                    else:
                        pe.wait_ge(zh_ready, K * t + (3 + s) // 2 + 1)
                    if first:
                        pe.wait_ge(w_lo_ready, 5)
                    tok = slice(s * P, (s + 1) * P)
                    three(pj_bank(FFN1 + s)[:, 0:F + NE],
                          [(xT_hi[:, k, tok], xT_lo[:, k, tok], w1_hi[:, k, :], w1_lo[:, k, :]) for k in range(K)],
                          ).then_inc(products_done, 1)
                turns = [lambda f=f: turn_hid(t, f) for f in range(KF)]
                if not last:
                    turns += [lambda k=k: turn_x(t + 1, k) for k in range(K)]
                for m in range(K):
                    if m == 0:
                        pe.wait_ge(zh_ready, K * t + K)
                    else:
                        pe.wait_ge(hid_ready, SB * t + m)
                    if first:
                        pe.wait_ge(w_lo_ready, 6)
                    col = slice(m * P, (m + 1) * P)
                    three(pj_bank(GATE + m)[:, :],
                          [(wg_hi[:, k, col], wg_lo[:, k, col], h_hi[:, k, :], h_lo[:, k, :]) for k in range(K)],
                          (lambda k: pe.wait_ge(h_lo_ready, K * t + k + 1)) if m == 0 else None,
                          ).then_inc(products_done, 1)
                    if turns:
                        turns.pop(0)()
                for s in range(SB):
                    if s == 0:
                        pe.wait_ge(hid_ready, SB * t + SB)
                        pe.wait_ge(turned_lo, hid_chunk(t, KF - 1) + 1)
                    else:
                        pe.wait_ge(gate_ready, K * t + s)
                    if first:
                        pe.wait_ge(w_lo_ready, 7)
                    tok = slice(s * P, (s + 1) * P)
                    pairs = [(hidT_hi[:, f, tok], hidT_lo[:, f, tok], w2_hi[:, f, :], w2_lo[:, f, :]) for f in range(KF)]
                    for i, (s_hi, s_lo, m_hi, m_lo) in enumerate(pairs):
                        for j, (st, mv) in enumerate(((s_hi, m_hi), (s_lo, m_hi), (s_hi, m_lo))):
                            pe.matmul(pj_bank(OUT + s)[:, :], st, mv, start=(i == 0 and j == 0), stop=(i == KF - 1 and j == 2))
                    if turns:
                        turns.pop(0)()
                pe.wait_ge(gated_ready, K * t + K)
                for s in range(SB):
                    for m in range(K):
                        mm = pe.matmul(pj_bank(OUT + s)[:, m * P:(m + 1) * P], gate[:, m, s * P:(s + 1) * P],
                                       ident[:, :], is_transpose=True, start=False, stop=True,
                                       skip_group_check=True)
                    mm.then_inc(sums_done, 1)

            pe.wait_ge(ident_ready, 1)
            pe.wait_ge(bias_loaded, 16 * 5)
            pe.transpose(pj[NPJ - 1][:, 0:3 * K], bias_rows[:, :], ident[0:3 * K, 0:3 * K]).then_inc(bias_turned, 1)
            for k in range(K):
                turn_x(0, k)
            tiles(pe, one_tile)
            pe.wait_ge(route_step, 3)
            pe.wait_ge(const_ready, 2)
            pe.matmul(tp[0][0:1, 0:1], n_ones[:, :], ones[:, :], start=True, stop=True).then_inc(counted, 1)

            pe.wait_ge(flag_ready, 1)
            routed = pe.value_load(flag[0:1, 0:1])
            with pe.If(routed > 0):
                pe.wait_ge(y_ready, SB * NT)
                pe.sem_inc(fb_y_done, 1)
                with pe.Fori(0, NT) as t:
                    pe.wait_ge(fb_xn_ready, (t + 1) * SB)
                    for k in range(K):
                        for s in range(SB):
                            mm = pe.transpose(pj[k][:, s * P:(s + 1) * P], xn[:, s, k * P:(k + 1) * P], ident[:, :])
                        mm.then_inc(fb_turned, 1)
                    with pe.Fori(0, NE) as e:
                        pe.wait_ge(fb_xT_ready, (t + 1) * K)
                        pe.wait_ge(fb_y_added, (t * NE + e) * SB + 1)
                        pe.wait_ge(fb_w_loaded, (t * NE + e + 1) * 32)
                        for s in range(SB):
                            for k in range(K):
                                mm = pe.matmul(pj[s][:, 0:F], fb_xT[:, k, s * P:(s + 1) * P], fb_w1[:, k, :],
                                               start=(k == 0), stop=(k == K - 1))
                            mm.then_inc(fb_hid_done, 1)
                        pe.wait_ge(fb_hid_ready, (t * NE + e + 1) * SB)
                        for f in range(KF):
                            for s in range(SB):
                                mm = pe.transpose(tp[f][:, s * P:(s + 1) * P], hid[:, s, f * P:(f + 1) * P], ident[:, :])
                            mm.then_inc(fb_hid_turned, 1)
                        pe.wait_ge(fb_hidT_ready, (t * NE + e + 1) * KF)
                        for s in range(SB):
                            for f in range(KF):
                                mm = pe.matmul(pj[s][:, :], fb_hidT[:, f, s * P:(s + 1) * P], fb_w2[:, f, :],
                                               start=(f == 0), stop=(f == KF - 1))
                            mm.then_inc(fb_y_done, 1)


_INS = ['L0_attn_x', 'L0_attn_W_zf', 'L0_attn_b_zf', 'L0_attn_W_hf', 'L0_attn_b_hf', 'L0_attn_W_zs', 'L0_attn_b_zs',
        'L0_attn_W_hs', 'L0_attn_b_hs', 'L0_attn_W_g', 'L0_attn_b_g', 'L0_ffn_Ws1', 'L0_ffn_Ws2', 'L0_ffn_W1',
        'L0_ffn_W2', 'L0_ffn_Wr']
_OUTS = [((1, 8192, 512), 'float32')]


def kernel(**inputs):
    import numpy as _np
    import concourse.bacc as _bacc
    from concourse import mybir as _mybir
    from concourse.bass_utils import run_bass_kernel_spmd as _run

    nc = _bacc.Bacc("TRN2", target_bir_lowering=False, num_devices=1)
    arrays, args = {}, []
    for name in _INS:
        a = _np.ascontiguousarray(inputs[name])
        arrays[f"in_{name}_dram"] = a
        args.append(nc.dram_tensor(f"in_{name}_dram", a.shape, _mybir.dt.from_np(a.dtype), kind="ExternalInput").ap())
    for i, (shape, dtype) in enumerate(_OUTS):
        dt = _mybir.dt.from_np(_np.dtype(dtype))
        args.append(nc.dram_tensor(f"out_{i}_dram", shape, dt, kind="ExternalOutput").ap())
    minlstm_gated_moe_kernel(nc, *args)
    r = _run(nc, [arrays], core_ids=[0])
    got = tuple(r.results[0][f"out_{i}_dram"] for i in range(len(_OUTS)))
    return got[0]
```

```python
from contextlib import ExitStack

import concourse.bass as bass
from concourse import mybir

F32 = mybir.dt.float32
F32R = mybir.dt.float32r
I32 = mybir.dt.int32
ALU = mybir.AluOpType
ACT = mybir.ActivationFunctionType
AX_X = mybir.AxisListType.X

P = 128
TOK = 512
SB = TOK // P
EPS = 1e-5


def minlstm_gated_moe_kernel(
    nc, x, w_zf, b_zf, w_hf, b_hf, w_zs, b_zs, w_hs, b_hs, w_g, b_g, w_s1, w_s2, w_e1, w_e2, w_r, out
):
    _, S, D = x.shape
    DF = w_zf.shape[1]
    F = w_s1.shape[1]
    NE = w_r.shape[1]
    NT = S // TOK
    NB = S // P
    K = D // P
    KF = F // P
    CF = DF // P
    assert 2 * DF == D and K == 4 and SB == 4 and KF == 2 and NT % 2 == 0 and S % TOK == 0
    Q = 32
    NQ = P // Q
    G = TOK // Q
    assert D == NQ * P and K == NQ
    NPJ = 5
    PU = 4 * K + SB

    x_v = x.rearrange("a (b p) d -> p (a b) d", p=P)
    out_v = out.rearrange("a (b p) d -> p (a b) d", p=P)
    x_quad = x.rearrange("a (b r) (q j) -> q r (a b) j", r=Q, q=NQ)
    out_quad = out.rearrange("a (b r) (q j) -> q r (a b) j", r=Q, q=NQ)

    ctx = ExitStack()
    with ctx:
        def sb(name, shape, dt=F32):
            return ctx.enter_context(nc.sbuf_tensor(name, shape, dt))

        def sem(name):
            return ctx.enter_context(nc.semaphore(name))

        wz_hi, wz_lo = sb("wz_hi", [P, K, D], F32R), sb("wz_lo", [P, K, D], F32R)
        wh_hi, wh_lo = sb("wh_hi", [P, K, D], F32R), sb("wh_lo", [P, K, D], F32R)
        wg_hi, wg_lo = sb("wg_hi", [P, K, D], F32R), sb("wg_lo", [P, K, D], F32R)
        w1_hi, w1_lo = sb("w1_hi", [P, K, F + NE], F32R), sb("w1_lo", [P, K, F + NE], F32R)
        w2_hi, w2_lo = sb("w2_hi", [P, KF, D], F32R), sb("w2_lo", [P, KF, D], F32R)
        wz_in, w2_in = sb("wz_in", [P, K, D])[:, :, :], sb("w2_in", [P, KF, D])[:, :, :]
        wr_in = sb("wr_in", [P, K, NE])[:, :, :]

        x_tok = sb("x_tok", [P, SB, D])
        x_q = sb("x_q", [P, 2, G, P])
        xn = sb("xn", [P, G, P])
        xT = sb("xT", [P, K, TOK])
        stats = sb("stats", [P, SB, 6])
        mean_rstd = sb("mean_rstd", [P, SB, 2])
        var_eps = sb("var_eps", [P, SB])
        minus_half = sb("minus_half", [P, SB])
        mean_rstd_q = sb("mean_rstd_q", [P, G, 2])
        mean_rstd_all = sb("mean_rstd_all", [P, NB, 2])
        xT_hi, xT_lo = sb("xT_hi", [P, K, TOK], F32R), sb("xT_lo", [P, K, TOK], F32R)
        z = sb("z", [P, 2, TOK])
        a = sb("a", [P, 2, TOK])
        zh = sb("zh", [P, 2, TOK])
        h = sb("h", [P, K, TOK])
        h_hi, h_lo = sb("h_hi", [P, K, TOK], F32R), sb("h_lo", [P, K, TOK], F32R)
        gate = sb("gate", [P, K, TOK])
        relu = sb("relu", [P, 2, F])
        hid = sb("hid", [P, SB, F])
        hidT_hi, hidT_lo = sb("hidT_hi", [P, KF, TOK], F32R), sb("hidT_lo", [P, KF, TOK], F32R)
        y = sb("y", [P, G, P])
        wg_in = gate[:, :, :]
        wh_in = y[:, :, :].rearrange("p (k a) b -> p k (a b)", k=K)
        w1_in = hid[:, :, :]

        bias = sb("bias", [P, 3 * K])
        neg_bz = sb("neg_bz", [P, K])
        ident = sb("ident", [P, P])
        ones = sb("ones", [P, 1])
        logits = sb("logits", [P, NB, NE])
        top8 = sb("top8", [P, SB, 8])
        top2 = sb("top2", [P, NB, 2])
        gap = sb("gap", [P, NB])
        expo = sb("expo", [P, NB])
        denom = sb("denom", [P, NB])
        is_one = sb("is_one", [P, NB])
        n_ones = sb("n_ones", [P, 1])
        flag = sb("flag", [1, 1], I32)
        prob = xT[:, 0, :].rearrange("p (b e) -> p b e", e=NE)

        pj = [ctx.enter_context(nc.psum_tensor(f"pj{i}", [P, TOK], F32)) for i in range(NPJ)]
        tp = [ctx.enter_context(nc.psum_tensor(f"tp{i}", [P, TOK], F32)) for i in range(KF)]

        x_loaded, xq_loaded = sem("x_loaded"), [sem(f"xq_loaded{i}") for i in range(2)]
        bias_loaded = sem("bias_loaded")
        W = ["zf", "hf", "zs", "hs", "w1", "g", "w2"]
        w_loaded = {n: sem(f"w_loaded_{n}") for n in W}
        w_hi = {n: sem(f"w_hi_{n}") for n in W}
        w_ready = {n: sem(f"w_ready_{n}") for n in W}
        ident_zeroed, ident_ready, const_ready = sem("ident_zeroed"), sem("ident_ready"), sem("const_ready")
        neg_bz_ready = sem("neg_bz_ready")
        stats_ready, mean_var_ready, var_eps_ready = sem("stats_ready"), sem("mean_var_ready"), sem("var_eps_ready")
        rstd_ready, ln_kept, spread_ready = sem("rstd_ready"), sem("ln_kept"), sem("spread_ready")
        xn_ready, xT_ready, xT_hi_ready, xT_lo_ready = (
            sem(n) for n in ("xn_ready", "xT_ready", "xT_hi_ready", "xT_lo_ready"))
        turned, turned_hi, turned_lo = sem("turned"), sem("turned_hi"), sem("turned_lo")
        products_done = sem("products_done")
        z_a_ready, zh_ready, scan_done = sem("z_a_ready"), sem("zh_ready"), sem("scan_done")
        h_hi_ready, h_lo_ready = sem("h_hi_ready"), sem("h_lo_ready")
        relu_ready, top8_ready, hid_ready = sem("relu_ready"), sem("top8_ready"), sem("hid_ready")
        top2_kept = sem("top2_kept")
        gate_ready, gated_ready = sem("gate_ready"), sem("gated_ready")
        sum_ready, y_turned, y_ready, y_stored = (
            sem(n) for n in ("sum_ready", "y_turned", "y_ready", "y_stored"))
        gap_ready, expo_ready, route_step = sem("gap_ready"), sem("expo_ready"), sem("route_step")
        counted, flag_ready = sem("counted"), sem("flag_ready")

        Z_H, FFN1, GATE, OUT = 0, 2 * K, 2 * K + SB, 2 * K + SB + K

        def pj_bank(u):
            return pj[u % NPJ]

        def reached(eng, semaphore, value):
            if not (isinstance(value, int) and value <= 0):
                eng.wait_ge(semaphore, value)

        def tiles(eng, one_tile):
            one_tile(0, 0)
            with eng.Fori(0, NT // 2 - 1) as i:
                one_tile(2 * i + 1, 1)
                one_tile(2 * i + 2, 0)
            one_tile(NT - 1, 1, last=True)

        fb_loaded, fb_xn_ready, fb_turned, fb_xT_ready = (
            sem(n) for n in ("fb_loaded", "fb_xn_ready", "fb_turned", "fb_xT_ready"))
        fb_w_loaded, fb_hid_done, fb_relu, fb_hid_ready = (
            sem(n) for n in ("fb_w_loaded", "fb_hid_done", "fb_relu", "fb_hid_ready"))
        fb_hid_turned, fb_hidT_ready, fb_y_done, fb_y_added = (
            sem(n) for n in ("fb_hid_turned", "fb_hidT_ready", "fb_y_done", "fb_y_added"))
        fb_route = sem("fb_route")
        fb_w1, fb_w2 = wz_in[:, :, 0:F], w2_in[:, :, :]
        fb_xT, fb_hidT = h, zh
        fb_xn = xn[:, :, :].rearrange("p (s a) b -> p s (a b)", s=SB)
        fb_y = y[:, :, :].rearrange("p (s a) b -> p s (a b)", s=SB)

        def load_rows(eng, dst, w, semaphore):
            eng.dma_start(dst, w.rearrange("(p j) f -> p j f", j=K)).then_inc(semaphore, 16)

        def half(w, w_in, n):
            return in_order(w)[:, :, :, n * P // 2:(n + 1) * P // 2], loaded(w_in)[:, :, :, n * P // 2:(n + 1) * P // 2]

        def in_order(w):
            return w[:, :, :].rearrange("p k (m c) -> p k m c", m=K)

        def loaded(w_in):
            return w_in.rearrange("p k (c m) -> p k m c", m=K)

        block = ctx.enter_context(nc.Block())

        @block.sync
        def _(sp):
            def load_quad(t, parity):
                for q in range(NQ):
                    sp.dma_start(x_q[q * Q:(q + 1) * Q, parity, :, :],
                                 x_quad[q, :, bass.ts(t, G), :]).then_inc(xq_loaded[parity], 16)

            sp.dma_start(x_tok[:, :, :], x_v[:, 0:SB, :]).then_inc(x_loaded, 16)
            load_quad(0, 0)
            load_rows(sp, wz_in[:, :, DF:D], w_zs, w_loaded["zs"])
            load_rows(sp, wh_in[:, :, DF:D], w_hs, w_loaded["hs"])
            sp.wait_ge(stats_ready, SB)
            sp.dma_start(x_tok[:, :, :], x_v[:, SB:2 * SB, :]).then_inc(x_loaded, 16)
            load_quad(1, 1)
            load_rows(sp, wg_in, w_g, w_loaded["g"])

            def load_tok(t):
                sp.wait_ge(stats_ready, SB * t)
                sp.dma_start(x_tok[:, :, :], x_v[:, bass.ts(t, SB), :]).then_inc(x_loaded, 16)

            def store(t):
                sp.wait_ge(y_ready, K * t + K)
                for q in range(NQ):
                    sp.dma_start(out_quad[q, :, bass.ts(t, G), :],
                                 y[q * Q:(q + 1) * Q, :, :]).then_inc(y_stored, 16)

            with sp.Fori(0, NT // 2 - 1) as i:
                for parity in range(2):
                    load_tok(2 * i + parity + 2)
                    store(2 * i + parity)
                    load_quad(2 * i + parity + 2, parity)
            store(NT - 2)
            store(NT - 1)
            sp.wait_ge(y_stored, 16 * NQ * NT)

            sp.wait_ge(flag_ready, 1)
            routed = sp.value_load(flag[0:1, 0:1])
            with sp.If(routed > 0):
                with sp.Fori(0, NT) as t:
                    sp.wait_ge(y_stored, t * 16 + 16 * NQ * NT)
                    sp.dma_start(x_tok[:, :, :], x_v[:, bass.ts(t, SB), :]).then_inc(fb_loaded, 16)
                    sp.dma_start(fb_y, out_v[:, bass.ts(t, SB), :]).then_inc(fb_loaded, 16)
                    with sp.Fori(0, NE) as e:
                        sp.wait_ge(fb_y_done, (t * NE + e) * SB + 1)
                        sp.dma_start(fb_w1, w_e1[bass.ds(e, 1), :, :].rearrange("a (k p) f -> p (a k) f", p=P)).then_inc(fb_w_loaded, 16)
                        sp.dma_start(fb_w2, w_e2[bass.ds(e, 1), :, :].rearrange("a (k p) f -> p (a k) f", p=P)).then_inc(fb_w_loaded, 16)
                    sp.wait_ge(fb_y_added, (t + 1) * (NE * SB) + 1)
                    sp.dma_start(out_v[:, bass.ts(t, SB), :], fb_y).then_inc(y_stored, 16)
                sp.wait_ge(y_stored, 16 * (NQ + 1) * NT)

        @block.gpsimd
        def _(pool):
            pool.memset(ident[:, :], 0.0).then_inc(ident_zeroed, 1)
            pool.memset(minus_half[:, :], -0.5).then_inc(const_ready, 1)
            pool.memset(ones[:, :], 1.0).then_inc(const_ready, 1)
            pool.wait_ge(ident_zeroed, 1)
            pool.affine_select(out=ident[:, :], in_=ident[:, :], compare_op=ALU.not_equal, fill=1.0,
                               base=0, pattern=[[-1, P]], channel_multiplier=1).then_inc(ident_ready, 1)
            load_rows(pool, w1_in, w_s1, w_loaded["w1"])
            load_rows(pool, wr_in, w_r, w_loaded["w1"])
            pool.dma_start(w2_in[:, :, :], w_s2.rearrange("(k p) f -> p k f", p=P)).then_inc(w_loaded["w2"], 16)

            def inverse_std(t):
                pool.wait_ge(var_eps_ready, t + 1)
                if isinstance(t, int) and t == 0:
                    pool.wait_ge(const_ready, 2)
                pool.tensor_tensor(mean_rstd[:, :, 1], var_eps[:, :], minus_half[:, :], ALU.pow).then_inc(rstd_ready, 1)

            def split_lo(n, lo, full, hi):
                pool.wait_ge(w_hi[n], 1)
                pool.tensor_tensor(lo, full, hi.bitcast(F32), ALU.subtract).then_inc(w_ready[n], 1)

            inverse_std(0)
            split_lo("zs", *half(wz_lo, wz_in, 1), half(wz_hi, wz_in, 1)[0])
            split_lo("hs", *half(wh_lo, wh_in, 1), half(wh_hi, wh_in, 1)[0])
            inverse_std(1)
            pool.wait_ge(w_hi["w1"], 1)
            pool.tensor_tensor(w1_lo[:, :, F:F + NE], wr_in[:, :, :], w1_hi[:, :, F:F + NE].bitcast(F32),
                               ALU.subtract).then_inc(w_ready["w1"], 1)
            split_lo("w1", w1_lo[:, :, 0:F], w1_in[:, :, :], w1_hi[:, :, 0:F])
            split_lo("g", in_order(wg_lo), loaded(wg_in), in_order(wg_hi))
            split_lo("w2", in_order(w2_lo), loaded(w2_in), in_order(w2_hi))
            with pool.Fori(2, NT) as t:
                inverse_std(t)

        @block.scalar
        def _(act):
            load_rows(act, wz_in[:, :, 0:DF], w_zf, w_loaded["zf"])
            load_rows(act, wh_in[:, :, 0:DF], w_hf, w_loaded["hf"])
            for col, b, row in ((0, b_zf, 0), (0, b_zs, P // 2), (K, b_hf, 0), (K, b_hs, P // 2), (2 * K, b_g, 0)):
                act.dma_start(bias[row:row + b.shape[0] // K, col:col + K],
                              b.rearrange("(p m) -> p m", m=K)).then_inc(bias_loaded, 16)

            def split_hi(n, hi, full, loads=1):
                act.wait_ge(w_loaded[n], 16 * loads)
                act.activation(hi, full, ACT.Copy).then_inc(w_hi[n], 1)

            def spread(t):
                act.wait_ge(rstd_ready, t + 1)
                reached(act, xn_ready, G * t)
                dst = mean_rstd_q[:, :, :].rearrange("p (s i) v -> p i s v", i=NQ)
                for i in range(NQ):
                    for q in range(NQ):
                        act.activation(dst[q * Q:(q + 1) * Q, i, :, :], mean_rstd[i * Q:(i + 1) * Q, :, :],
                                       ACT.Copy).then_inc(spread_ready, 1)

            def xT_hi_part(t, k):
                act.wait_ge(xT_ready, K * t + k + 1)
                reached(act, products_done, PU * t - PU + GATE)
                act.activation(xT_hi[:, k, :], xT[:, k, :], ACT.Copy).then_inc(xT_hi_ready, 1)

            def turned_hi_part(t, f):
                act.wait_ge(turned, KF * t + f + 1)
                act.activation(hidT_hi[:, f, :], tp[f][:, :], ACT.Copy).then_inc(turned_hi, 1)

            split_hi("zf", *half(wz_hi, wz_in, 0))
            spread(0)
            split_hi("hf", *half(wh_hi, wh_in, 0))
            for k in range(K):
                xT_hi_part(0, k)
            split_hi("zs", *half(wz_hi, wz_in, 1))
            split_hi("hs", *half(wh_hi, wh_in, 1))

            def one_tile(t, parity, last=False):
                for c in range(K):
                    act.wait_ge(products_done, PU * t + 2 * c + 1)
                    reached(act, scan_done, K * t + c - 1)
                    if isinstance(t, int) and t == 0 and c == 0:
                        act.wait_ge(neg_bz_ready, 1)
                    u = pj_bank(Z_H + 2 * c)
                    act.activation(z[:, c % 2, :], u[:, :], ACT.Sigmoid, bias=bias[:, c:c + 1]).then_inc(z_a_ready, 1)
                    act.activation(a[:, c % 2, :], u[:, :], ACT.Sigmoid, bias=neg_bz[:, c:c + 1], scale=-1.0).then_inc(z_a_ready, 1)
                    if c:
                        hi_part(t, c - 1)
                    if isinstance(t, int) and t == 0 and c == 0:
                        act.wait_ge(w_loaded["w1"], 16 * 2)
                        act.activation(w1_hi[:, :, F:F + NE], wr_in[:, :, :], ACT.Copy)
                        split_hi("w1", w1_hi[:, :, 0:F], w1_in[:, :, :], loads=2)
                    if isinstance(t, int) and t == 0 and c == 1:
                        split_hi("g", in_order(wg_hi), loaded(wg_in))
                    if isinstance(t, int) and t == 0 and c == 2:
                        split_hi("w2", in_order(w2_hi), loaded(w2_in))
                    if c == 1 and not last:
                        spread(t + 1)
                for s in range(SB):
                    act.wait_ge(products_done, PU * t + FFN1 + s + 1)
                    reached(act, hid_ready, SB * t + s - 1)
                    act.activation(relu[:, s % 2, :], pj_bank(FFN1 + s)[:, 0:F], ACT.Relu).then_inc(relu_ready, 1)
                    if s == 1:
                        hi_part(t, K - 1)
                for m in range(K):
                    act.wait_ge(products_done, PU * t + GATE + m + 1)
                    if m == 0:
                        reached(act, y_turned, K * t)
                    act.activation(gate[:, m, :], pj_bank(GATE + m)[:, :], ACT.Sigmoid,
                                   bias=bias[:, 2 * K + m:2 * K + m + 1]).then_inc(gate_ready, 1)
                    if m < KF:
                        turned_hi_part(t, m)
                    if not last:
                        xT_hi_part(t + 1, m)

            def hi_part(t, c):
                act.wait_ge(scan_done, K * t + c + 1)
                act.activation(h_hi[:, c, :], h[:, c, :], ACT.Copy).then_inc(h_hi_ready, 1)

            tiles(act, one_tile)
            act.wait_ge(gap_ready, 1)
            act.activation(expo[:, :], gap[:, :], ACT.Exp).then_inc(expo_ready, 1)

        @block.vector
        def _(dve):
            def ln_stats(t):
                dve.wait_ge(x_loaded, 16 * t + 16)
                reached(dve, mean_var_ready, SB * t)
                for s in range(SB):
                    dve.bn_stats(stats[:, s, :], x_tok[:, s, :]).then_inc(stats_ready, 1)

            def ln_stats_done(t):
                dve.wait_ge(stats_ready, SB * t + SB)
                reached(dve, ln_kept, t)
                reached(dve, spread_ready, NQ * NQ * t)

            def ln_mean_var(t):
                for s in range(SB):
                    dve.bn_aggr(mean_rstd[:, s, :], stats[:, s, :]).then_inc(mean_var_ready, 1)
                dve.wait_ge(mean_var_ready, SB * t + SB)
                dve.tensor_scalar(var_eps[:, :], mean_rstd[:, :, 1], EPS, None, ALU.add).then_inc(var_eps_ready, 1)

            def ln_apply(t, parity, groups):
                dve.wait_ge(xq_loaded[parity], 8 * NQ * (t - parity) + 16 * NQ)
                dve.wait_ge(spread_ready, NQ * NQ * t + NQ * NQ)
                reached(dve, xT_ready, K * t)
                if groups[0] == 0:
                    dve.tensor_copy(mean_rstd_all[:, bass.ts(t, SB), :], mean_rstd[:, :, :]).then_inc(ln_kept, 1)
                for g in groups:
                    dve.tensor_scalar(xn[:, g, :], x_q[:, parity, g, :], mean_rstd_q[:, g, 0:1],
                                      mean_rstd_q[:, g, 1:2], ALU.subtract, ALU.mult).then_inc(xn_ready, 1)

            def turn_x(t, j):
                dve.wait_ge(xn_ready, G * t + G)
                reached(dve, xT_lo_ready, K * t - K + j + 1)
                dve.transpose(xT[:, j, :].rearrange("p (g r) -> p g r", r=Q),
                              xn[:, :, j::K]).then_inc(xT_ready, 1)

            def xT_lo_part(t, k):
                dve.wait_ge(xT_hi_ready, K * t + k + 1)
                dve.tensor_tensor(xT_lo[:, k, :], xT[:, k, :], xT_hi[:, k, :].bitcast(F32),
                                  ALU.subtract).then_inc(xT_lo_ready, 1)

            def turned_lo_part(t, f):
                dve.wait_ge(turned_hi, KF * t + f + 1)
                dve.tensor_tensor(hidT_lo[:, f, :], tp[f][:, :], hidT_hi[:, f, :].bitcast(F32),
                                  ALU.subtract).then_inc(turned_lo, 1)

            def lo_part(t, c):
                dve.wait_ge(h_hi_ready, K * t + c + 1)
                dve.tensor_tensor(h_lo[:, c, :], h[:, c, :], h_hi[:, c, :].bitcast(F32),
                                  ALU.subtract).then_inc(h_lo_ready, 1)

            def one_tile(t, parity, last=False):
                first = isinstance(t, int) and t == 0
                for c in range(K):
                    dve.wait_ge(z_a_ready, 2 * (K * t + c) + 1)
                    dve.wait_ge(products_done, PU * t + 2 * c + 2)
                    reached(dve, scan_done, K * t + c - 1)
                    dve.scalar_tensor_tensor(zh[:, c % 2, :], pj_bank(Z_H + 2 * c + 1)[:, :], bias[:, K + c:K + c + 1],
                                             z[:, c % 2, :], ALU.add, ALU.mult).then_inc(zh_ready, 1)
                    if c:
                        lo_part(t, c - 1)
                    elif not last:
                        ln_stats(t + 1)
                    dve.wait_ge(z_a_ready, 2 * (K * t + c) + 2)
                    dve.wait_ge(zh_ready, K * t + c + 1)
                    reached(dve, gated_ready, K * t)
                    if c == 0 and not last:
                        ln_stats_done(t + 1)
                    dve.tensor_tensor_scan(h[:, c, :], a[:, c % 2, :], zh[:, c % 2, :],
                                           0.0 if first else h[:, c, TOK - 1:TOK],
                                           ALU.mult, ALU.add).then_inc(scan_done, 1)
                    if not last:
                        if c == 0:
                            ln_mean_var(t + 1)
                        if c >= 2:
                            ln_apply(t + 1, 1 - parity, range((c - 2) * G // 2, (c - 1) * G // 2))
                for s in range(SB):
                    bank = pj_bank(FFN1 + s)
                    dve.wait_ge(relu_ready, SB * t + s + 1)
                    if s == 0:
                        reached(dve, top2_kept, t)
                    dve.tensor_copy(logits[:, bass.ds(t * SB + s, 1), :], bank[:, F:F + NE].rearrange("p (a e) -> p a e", a=1))
                    dve.max(top8[:, s, :], bank[:, F:F + NE]).then_inc(top8_ready, 1)
                    dve.tensor_tensor(hid[:, s, :], bank[:, 0:F], relu[:, s % 2, :], ALU.mult).then_inc(hid_ready, 1)
                    if s == 1:
                        lo_part(t, K - 1)
                dve.wait_ge(top8_ready, SB * t + SB)
                dve.tensor_copy(top2[:, bass.ts(t, SB), :], top8[:, :, 0:2]).then_inc(top2_kept, 1)
                if last:
                    dve.wait_ge(top2_kept, NT)
                    dve.tensor_tensor(gap[:, :], top2[:, :, 1], top2[:, :, 0], ALU.subtract).then_inc(gap_ready, 1)
                if not last:
                    turn_x(t + 1, 0)
                    turn_x(t + 1, 1)
                for m in range(K):
                    if m < KF:
                        turned_lo_part(t, m)
                    dve.wait_ge(gate_ready, K * t + m + 1)
                    dve.tensor_tensor(gate[:, m, :], gate[:, m, :], h[:, m, :], ALU.mult).then_inc(gated_ready, 1)
                    if not last:
                        if m + 2 < K:
                            turn_x(t + 1, m + 2)
                        xT_lo_part(t + 1, m)
                for step in range(K + 2):
                    if step < K:
                        m = step
                        dve.wait_ge(products_done, PU * t + OUT + m + 1)
                        dve.wait_ge(gated_ready, K * t + m + 1)
                        dve.tensor_tensor(gate[:, m, :], pj_bank(OUT + m)[:, :], gate[:, m, :], ALU.add).then_inc(sum_ready, 1)
                    if 1 <= step <= K:
                        m = step - 1
                        if m == 0:
                            reached(dve, y_stored, 16 * NQ * t)
                        dve.wait_ge(sum_ready, K * t + m + 1)
                        dve.transpose(y[:, :, m::K],
                                      gate[:, m, :].rearrange("p (g r) -> p g r", r=Q)).then_inc(y_turned, 1)
                    if step >= 2:
                        m = step - 2
                        cols = slice(m, P, K)
                        dve.wait_ge(y_turned, K * t + m + 1)
                        dve.tensor_tensor(y[:, :, cols], y[:, :, cols], x_q[:, parity, :, cols], ALU.add).then_inc(y_ready, 1)

            def split_lo(n, lo, full, hi):
                dve.wait_ge(w_hi[n], 1)
                dve.tensor_tensor(lo, full, hi.bitcast(F32), ALU.subtract).then_inc(w_ready[n], 1)

            ln_stats(0)
            ln_stats_done(0)
            ln_mean_var(0)
            dve.wait_ge(bias_loaded, 16 * 5)
            dve.tensor_scalar(neg_bz[:, :], bias[:, 0:K], -1.0, None, ALU.mult).then_inc(neg_bz_ready, 1)
            split_lo("zf", *half(wz_lo, wz_in, 0), half(wz_hi, wz_in, 0)[0])
            ln_apply(0, 0, range(G))
            for k in range(K):
                turn_x(0, k)
            for k in range(K):
                xT_lo_part(0, k)
            split_lo("hf", *half(wh_lo, wh_in, 0), half(wh_hi, wh_in, 0)[0])
            tiles(dve, one_tile)

            dve.wait_ge(expo_ready, 1)
            dve.tensor_scalar(denom[:, :], expo[:, :], 1.0, None, ALU.add).then_inc(route_step, 1)
            dve.wait_ge(route_step, 1)
            dve.tensor_scalar(is_one[:, :], denom[:, :], 1.0, None, ALU.is_le).then_inc(route_step, 1)
            dve.wait_ge(route_step, 2)
            dve.tensor_reduce(n_ones[:, :], is_one[:, :], AX_X, ALU.add).then_inc(route_step, 1)
            dve.wait_ge(counted, 1)
            dve.tensor_copy(flag[:, :], tp[0][0:1, 0:1]).then_inc(flag_ready, 1)

            dve.wait_ge(flag_ready, 1)
            routed = dve.value_load(flag[0:1, 0:1])
            with dve.If(routed > 0):
                top1 = top2[:, :, 0:1].to_broadcast([P, NB, NE])
                dve.tensor_tensor(prob, logits[:, :, :], top1, ALU.is_equal).then_inc(fb_route, 1)
                dve.wait_ge(fb_route, 1)
                ones_b = is_one[:, :].rearrange("p (b a) -> p b a", a=1).to_broadcast([P, NB, NE])
                dve.tensor_tensor(prob, prob, ones_b, ALU.mult).then_inc(fb_route, 1)
                dve.wait_ge(fb_route, 2)
                prob_flat = xT[:, 0, :]
                mean_rstd_flat = mean_rstd_all[:, :, :].rearrange("p b v -> p (b v)")
                dve.sem_inc(fb_y_added, 1)
                with dve.Fori(0, NT) as t:
                    dve.wait_ge(fb_loaded, (t + 1) * 32)
                    for s in range(SB):
                        dve.tensor_scalar(fb_xn[:, s, :], x_tok[:, s, :], mean_rstd_flat[:, bass.ds(t * (2 * SB) + 2 * s, 1)],
                                          mean_rstd_flat[:, bass.ds(t * (2 * SB) + 2 * s + 1, 1)],
                                          ALU.subtract, ALU.mult).then_inc(fb_xn_ready, 1)
                    for k in range(K):
                        dve.wait_ge(fb_turned, t * K + k + 1)
                        dve.tensor_copy(fb_xT[:, k, :], pj[k][:, :]).then_inc(fb_xT_ready, 1)
                    with dve.Fori(0, NE) as e:
                        for s in range(SB):
                            dve.wait_ge(fb_hid_done, (t * NE + e) * SB + s + 1)
                            dve.tensor_scalar(relu[:, 0, :], pj[s][:, 0:F], 0.0, None, ALU.max).then_inc(fb_relu, 1)
                            dve.wait_ge(fb_relu, (t * NE + e) * SB + s + 1)
                            dve.scalar_tensor_tensor(hid[:, s, :], pj[s][:, 0:F],
                                                     prob_flat[:, bass.ds(t * (SB * NE) + s * NE + e, 1)],
                                                     relu[:, 0, :], ALU.mult, ALU.mult).then_inc(fb_hid_ready, 1)
                            dve.wait_ge(fb_hid_ready, (t * NE + e) * SB + s + 1)
                        for f in range(KF):
                            dve.wait_ge(fb_hid_turned, (t * NE + e) * KF + f + 1)
                            dve.tensor_copy(fb_hidT[:, f, :], tp[f][:, :]).then_inc(fb_hidT_ready, 1)
                        for s in range(SB):
                            dve.wait_ge(fb_y_done, (t * NE + e) * SB + s + 2)
                            dve.tensor_tensor(fb_y[:, s, :], pj[s][:, :], fb_y[:, s, :], ALU.add).then_inc(fb_y_added, 1)
                        dve.wait_ge(fb_y_added, (t * NE + e + 1) * SB + 1)

        @block.tensor
        def _(pe):
            def three(dst, pairs, hook=None):
                for i, (s_hi, s_lo, m_hi, m_lo) in enumerate(pairs):
                    if hook:
                        hook(i)
                    for j, (st, mv) in enumerate(((s_hi, m_hi), (s_lo, m_hi), (s_hi, m_lo))):
                        end = i == len(pairs) - 1 and j == 2
                        mm = pe.matmul(dst, st, mv, start=(i == 0 and j == 0), stop=end)
                return mm

            def turn(bank, sources):
                for s, src in enumerate(sources):
                    mm = pe.transpose(bank[:, s * P:(s + 1) * P], src, ident[:, :])
                mm.then_inc(turned, 1)

            def turn_hid(t, f):
                if f == 0:
                    pe.wait_ge(hid_ready, SB * t + SB)
                reached(pe, turned_lo, KF * t - KF + f + 1)
                turn(tp[f], [hid[:, s, f * P:(f + 1) * P] for s in range(SB)])

            def columns(w, k, m):
                return w[:, k, m * P:(m + 1) * P]

            def one_tile(t, parity, last=False):
                first = isinstance(t, int) and t == 0

                for c in range(K):
                    for kind, (whi, wlo) in enumerate(((wz_hi, wz_lo), (wh_hi, wh_lo))):
                        u = 2 * c + kind
                        if u == 0:
                            reached(pe, gate_ready, K * t)
                        elif u < NPJ:
                            reached(pe, sum_ready, K * t - K + u)
                        elif u % 2 == 1:
                            pe.wait_ge(z_a_ready, 2 * (K * t + (u - NPJ) // 2) + 2)
                        else:
                            pe.wait_ge(zh_ready, K * t + (u - NPJ) // 2 + 1)
                        if first:
                            for half in "fs":
                                pe.wait_ge(w_ready["zh"[kind] + half], 1)
                        three(pj_bank(u)[:, :],
                              [(columns(whi, k, c), columns(wlo, k, c), xT_hi[:, k, :], xT_lo[:, k, :]) for k in range(K)],
                              (lambda k: pe.wait_ge(xT_lo_ready, K * t + k + 1)) if u == 0 else None,
                              ).then_inc(products_done, 1)
                for s in range(SB):
                    if s % 2:
                        pe.wait_ge(z_a_ready, 2 * (K * t + (3 + s) // 2) + 2)
                    else:
                        pe.wait_ge(zh_ready, K * t + (3 + s) // 2 + 1)
                    if first:
                        pe.wait_ge(w_ready["w1"], 2)
                    tok = slice(s * P, (s + 1) * P)
                    three(pj_bank(FFN1 + s)[:, 0:F + NE],
                          [(xT_hi[:, k, tok], xT_lo[:, k, tok], w1_hi[:, k, :], w1_lo[:, k, :]) for k in range(K)],
                          ).then_inc(products_done, 1)
                for m in range(K):
                    if m == 0:
                        pe.wait_ge(zh_ready, K * t + K)
                    else:
                        pe.wait_ge(hid_ready, SB * t + m)
                    if first:
                        pe.wait_ge(w_ready["g"], 1)
                    three(pj_bank(GATE + m)[:, :],
                          [(columns(wg_hi, k, m), columns(wg_lo, k, m), h_hi[:, k, :], h_lo[:, k, :]) for k in range(K)],
                          (lambda k: pe.wait_ge(h_lo_ready, K * t + k + 1)) if m == 0 else None,
                          ).then_inc(products_done, 1)
                    if m < KF:
                        turn_hid(t, m)
                for m in range(K):
                    if m == 0:
                        pe.wait_ge(hid_ready, SB * t + SB)
                        pe.wait_ge(turned_lo, KF * t + KF)
                    else:
                        pe.wait_ge(gate_ready, K * t + m)
                    if first:
                        pe.wait_ge(w_ready["w2"], 1)
                    three(pj_bank(OUT + m)[:, :],
                          [(columns(w2_hi, f, m), columns(w2_lo, f, m), hidT_hi[:, f, :], hidT_lo[:, f, :]) for f in range(KF)],
                          ).then_inc(products_done, 1)

            pe.wait_ge(ident_ready, 1)
            tiles(pe, one_tile)
            pe.wait_ge(route_step, 3)
            pe.wait_ge(const_ready, 2)
            pe.matmul(tp[0][0:1, 0:1], n_ones[:, :], ones[:, :], start=True, stop=True).then_inc(counted, 1)

            pe.wait_ge(flag_ready, 1)
            routed = pe.value_load(flag[0:1, 0:1])
            with pe.If(routed > 0):
                pe.wait_ge(sum_ready, K * NT)
                pe.sem_inc(fb_y_done, 1)
                with pe.Fori(0, NT) as t:
                    pe.wait_ge(fb_xn_ready, (t + 1) * SB)
                    for k in range(K):
                        for s in range(SB):
                            mm = pe.transpose(pj[k][:, s * P:(s + 1) * P], fb_xn[:, s, k * P:(k + 1) * P], ident[:, :])
                        mm.then_inc(fb_turned, 1)
                    with pe.Fori(0, NE) as e:
                        pe.wait_ge(fb_xT_ready, (t + 1) * K)
                        pe.wait_ge(fb_y_added, (t * NE + e) * SB + 1)
                        pe.wait_ge(fb_w_loaded, (t * NE + e + 1) * 32)
                        for s in range(SB):
                            for k in range(K):
                                mm = pe.matmul(pj[s][:, 0:F], fb_xT[:, k, s * P:(s + 1) * P], fb_w1[:, k, :],
                                               start=(k == 0), stop=(k == K - 1))
                            mm.then_inc(fb_hid_done, 1)
                        pe.wait_ge(fb_hid_ready, (t * NE + e + 1) * SB)
                        for f in range(KF):
                            for s in range(SB):
                                mm = pe.transpose(tp[f][:, s * P:(s + 1) * P], hid[:, s, f * P:(f + 1) * P], ident[:, :])
                            mm.then_inc(fb_hid_turned, 1)
                        pe.wait_ge(fb_hidT_ready, (t * NE + e + 1) * KF)
                        for s in range(SB):
                            for f in range(KF):
                                mm = pe.matmul(pj[s][:, :], fb_hidT[:, f, s * P:(s + 1) * P], fb_w2[:, f, :],
                                               start=(f == 0), stop=(f == KF - 1))
                            mm.then_inc(fb_y_done, 1)


_INS = ['L0_attn_x', 'L0_attn_W_zf', 'L0_attn_b_zf', 'L0_attn_W_hf', 'L0_attn_b_hf', 'L0_attn_W_zs', 'L0_attn_b_zs',
        'L0_attn_W_hs', 'L0_attn_b_hs', 'L0_attn_W_g', 'L0_attn_b_g', 'L0_ffn_Ws1', 'L0_ffn_Ws2', 'L0_ffn_W1',
        'L0_ffn_W2', 'L0_ffn_Wr']
_OUTS = [((1, 8192, 512), 'float32')]


def kernel(**inputs):
    import numpy as _np
    import concourse.bacc as _bacc
    from concourse import mybir as _mybir
    from concourse.bass_utils import run_bass_kernel_spmd as _run

    nc = _bacc.Bacc("TRN2", target_bir_lowering=False, num_devices=1)
    arrays, args = {}, []
    for name in _INS:
        a = _np.ascontiguousarray(inputs[name])
        arrays[f"in_{name}_dram"] = a
        args.append(nc.dram_tensor(f"in_{name}_dram", a.shape, _mybir.dt.from_np(a.dtype), kind="ExternalInput").ap())
    for i, (shape, dtype) in enumerate(_OUTS):
        dt = _mybir.dt.from_np(_np.dtype(dtype))
        args.append(nc.dram_tensor(f"out_{i}_dram", shape, dt, kind="ExternalOutput").ap())
    minlstm_gated_moe_kernel(nc, *args)
    r = _run(nc, [arrays], core_ids=[0])
    got = tuple(r.results[0][f"out_{i}_dram"] for i in range(len(_OUTS)))
    return got[0]
```

```python
from contextlib import ExitStack

import concourse.bass as bass
from concourse import mybir

F32 = mybir.dt.float32
F32R = mybir.dt.float32r
I32 = mybir.dt.int32
ALU = mybir.AluOpType
ACT = mybir.ActivationFunctionType
AX_X = mybir.AxisListType.X

P = 128
TOK = 512
SB = TOK // P
EPS = 1e-5


def minlstm_gated_moe_kernel(
    nc, x, w_zf, b_zf, w_hf, b_hf, w_zs, b_zs, w_hs, b_hs, w_g, b_g, w_s1, w_s2, w_e1, w_e2, w_r, out
):
    _, S, D = x.shape
    DF = w_zf.shape[1]
    F = w_s1.shape[1]
    NE = w_r.shape[1]
    NT = S // TOK
    NB = S // P
    K = D // P
    KF = F // P
    assert 2 * DF == D and K == 4 and SB == 4 and KF == 2 and NT % 2 == 0 and S % TOK == 0
    Q = 32
    NQ = P // Q
    G = TOK // Q
    assert D == NQ * P and K == NQ
    NPJ = 5
    PU = 4 * K + SB

    x_v = x.rearrange("a (b p) d -> p (a b) d", p=P)
    out_v = out.rearrange("a (b p) d -> p (a b) d", p=P)
    x_quad = x.rearrange("a (b r) (q j) -> q r (a b) j", r=Q, q=NQ)
    out_quad = out.rearrange("a (b r) (q j) -> q r (a b) j", r=Q, q=NQ)

    ctx = ExitStack()
    with ctx:
        def sb(name, shape, dt=F32):
            return ctx.enter_context(nc.sbuf_tensor(name, shape, dt))

        def sem(name):
            return ctx.enter_context(nc.semaphore(name))

        wz_hi, wz_lo = sb("wz_hi", [P, K, D], F32R), sb("wz_lo", [P, K, D], F32R)
        wh_hi, wh_lo = sb("wh_hi", [P, K, D], F32R), sb("wh_lo", [P, K, D], F32R)
        wg_hi, wg_lo = sb("wg_hi", [P, K, D], F32R), sb("wg_lo", [P, K, D], F32R)
        w1_hi, w1_lo = sb("w1_hi", [P, K, F + NE], F32R), sb("w1_lo", [P, K, F + NE], F32R)
        w2_hi, w2_lo = sb("w2_hi", [P, KF, D], F32R), sb("w2_lo", [P, KF, D], F32R)
        wz_in, w2_in = sb("wz_in", [P, K, D])[:, :, :], sb("w2_in", [P, KF, D])[:, :, :]
        wr_in = sb("wr_in", [P, K, NE])[:, :, :]

        x_tok = sb("x_tok", [P, SB, D])
        x_q = sb("x_q", [P, 2, G, P])
        xn = sb("xn", [P, G, P])
        xn_tok = xn[:, :, :].rearrange("p (s a) b -> p s (a b)", s=SB)
        xT = sb("xT", [P, K, TOK])
        stats = sb("stats", [P, SB, 6])
        mean_rstd = sb("mean_rstd", [P, SB, 2])
        var_eps = sb("var_eps", [P, SB])
        minus_half = sb("minus_half", [P, SB])
        mean_rstd_q = sb("mean_rstd_q", [P, G, 2])
        mean_rstd_all = sb("mean_rstd_all", [P, NB, 2])
        xT_hi, xT_lo = sb("xT_hi", [P, K, TOK], F32R), sb("xT_lo", [P, K, TOK], F32R)
        z = sb("z", [P, 2, TOK])
        a = sb("a", [P, 2, TOK])
        zh = sb("zh", [P, 2, TOK])
        h = sb("h", [P, K, TOK])
        h_hi, h_lo = sb("h_hi", [P, K, TOK], F32R), sb("h_lo", [P, K, TOK], F32R)
        gate = sb("gate", [P, K, TOK])
        relu = sb("relu", [P, 2, F])
        hid = sb("hid", [P, SB, F])
        hidT_hi, hidT_lo = sb("hidT_hi", [P, KF, TOK], F32R), sb("hidT_lo", [P, KF, TOK], F32R)
        y = sb("y", [P, G, P])
        wg_in = gate[:, :, :]
        wh_in = y[:, :, :].rearrange("p (k a) b -> p k (a b)", k=K)
        w1_in = hid[:, :, :]

        bias = sb("bias", [P, 3 * K])
        neg_bz = sb("neg_bz", [P, K])
        ident = sb("ident", [P, P])
        ones = sb("ones", [P, 1])
        logits = sb("logits", [P, NB, NE])
        top8 = sb("top8", [P, SB, 8])
        top2 = sb("top2", [P, NB, 2])
        gap = sb("gap", [P, NB])
        expo = sb("expo", [P, NB])
        denom = sb("denom", [P, NB])
        is_one = sb("is_one", [P, NB])
        n_ones = sb("n_ones", [P, 1])
        flag = sb("flag", [1, 1], I32)
        prob = xT[:, 0, :].rearrange("p (b e) -> p b e", e=NE)

        pj = [ctx.enter_context(nc.psum_tensor(f"pj{i}", [P, TOK], F32)) for i in range(NPJ)]
        tp = [ctx.enter_context(nc.psum_tensor(f"tp{i}", [P, TOK], F32)) for i in range(KF)]

        x0_loaded = [sem(f"x0_loaded{s}") for s in range(SB)]
        x_loaded, xq_loaded = sem("x_loaded"), [sem(f"xq_loaded{i}") for i in range(2)]
        bias_loaded = sem("bias_loaded")
        W = ["zf", "hf", "zs", "hs", "w1", "g", "w2"]
        w_loaded = {n: sem(f"w_loaded_{n}") for n in W}
        w_hi = {n: sem(f"w_hi_{n}") for n in W}
        w_ready = {n: sem(f"w_ready_{n}") for n in W}
        ident_zeroed, ident_ready, const_ready = sem("ident_zeroed"), sem("ident_ready"), sem("const_ready")
        neg_bz_ready = sem("neg_bz_ready")
        stats_ready, mean_var_ready, var_eps_ready = sem("stats_ready"), sem("mean_var_ready"), sem("var_eps_ready")
        rstd_ready, ln_kept, spread_ready = sem("rstd_ready"), sem("ln_kept"), sem("spread_ready")
        xn_ready, xT_ready, xT_hi_ready, xT_lo_ready = (
            sem(n) for n in ("xn_ready", "xT_ready", "xT_hi_ready", "xT_lo_ready"))
        turned, turned_hi, turned_lo = sem("turned"), sem("turned_hi"), sem("turned_lo")
        products_done = sem("products_done")
        z_a_ready, zh_ready, scan_done = sem("z_a_ready"), sem("zh_ready"), sem("scan_done")
        h_hi_ready, h_lo_ready = sem("h_hi_ready"), sem("h_lo_ready")
        relu_ready, top8_ready, hid_ready = sem("relu_ready"), sem("top8_ready"), sem("hid_ready")
        top2_kept = sem("top2_kept")
        gate_ready, gated_ready = sem("gate_ready"), sem("gated_ready")
        sum_ready, y_turned, y_ready, y_stored = (
            sem(n) for n in ("sum_ready", "y_turned", "y_ready", "y_stored"))
        gap_ready, expo_ready, route_step = sem("gap_ready"), sem("expo_ready"), sem("route_step")
        counted, flag_ready = sem("counted"), sem("flag_ready")

        Z_H, FFN1 = 0, 2 * K
        GATE = [12, 13, 15, 17]
        OUT = [14, 16, 18, 19]
        FFN1_DONE = FFN1 + SB

        def pj_bank(u):
            return pj[u % NPJ]

        def reached(eng, semaphore, value):
            if not (isinstance(value, int) and value <= 0):
                eng.wait_ge(semaphore, value)

        def tiles(eng, one_tile):
            one_tile(0, 0)
            with eng.Fori(0, NT // 2 - 1) as i:
                one_tile(2 * i + 1, 1)
                one_tile(2 * i + 2, 0)
            one_tile(NT - 1, 1, last=True)

        fb_loaded, fb_xn_ready, fb_turned, fb_xT_ready = (
            sem(n) for n in ("fb_loaded", "fb_xn_ready", "fb_turned", "fb_xT_ready"))
        fb_w_loaded, fb_hid_done, fb_relu, fb_hid_ready = (
            sem(n) for n in ("fb_w_loaded", "fb_hid_done", "fb_relu", "fb_hid_ready"))
        fb_hid_turned, fb_hidT_ready, fb_y_done, fb_y_added = (
            sem(n) for n in ("fb_hid_turned", "fb_hidT_ready", "fb_y_done", "fb_y_added"))
        fb_route = sem("fb_route")
        fb_w1, fb_w2 = wz_in[:, :, 0:F], w2_in[:, :, :]
        fb_xT, fb_hidT = h, zh
        fb_y = y[:, :, :].rearrange("p (s a) b -> p s (a b)", s=SB)

        def xT_turned(t, k):
            return pj[k + 1][:, :] if isinstance(t, int) and t == 0 else xT[:, k, :]

        def load_rows(eng, dst, w, semaphore):
            eng.dma_start(dst, w.rearrange("(p j) f -> p j f", j=K)).then_inc(semaphore, 16)

        def half(w, w_in, n):
            return in_order(w)[:, :, :, n * P // 2:(n + 1) * P // 2], loaded(w_in)[:, :, :, n * P // 2:(n + 1) * P // 2]

        def in_order(w):
            return w[:, :, :].rearrange("p k (m c) -> p k m c", m=K)

        def loaded(w_in):
            return w_in.rearrange("p k (c m) -> p k m c", m=K)

        def spread(eng, copy, t):
            eng.wait_ge(rstd_ready, t + SB)
            reached(eng, xn_ready, G * t)
            dst = mean_rstd_q[:, :, :].rearrange("p (s i) v -> p i s v", i=NQ)
            for i in range(NQ):
                for q in range(NQ):
                    copy(dst[q * Q:(q + 1) * Q, i, :, :], mean_rstd[i * Q:(i + 1) * Q, :, :]).then_inc(spread_ready, 1)

        block = ctx.enter_context(nc.Block())

        @block.sync
        def _(sp):
            def load_quad(t, parity):
                for q in range(NQ):
                    sp.dma_start(x_q[q * Q:(q + 1) * Q, parity, :, :],
                                 x_quad[q, :, bass.ts(t, G), :]).then_inc(xq_loaded[parity], 16)

            for s in range(SB):
                sp.dma_start(x_tok[:, s, :], x_v[:, s, :]).then_inc(x0_loaded[s], 16)
            load_rows(sp, wz_in[:, :, 0:DF], w_zf, w_loaded["zf"])
            load_rows(sp, wz_in[:, :, DF:D], w_zs, w_loaded["zs"])
            load_rows(sp, wh_in[:, :, 0:DF], w_hf, w_loaded["hf"])
            load_rows(sp, wh_in[:, :, DF:D], w_hs, w_loaded["hs"])
            sp.wait_ge(xn_ready, G)
            sp.dma_start(x_tok[:, :, :], x_v[:, SB:2 * SB, :]).then_inc(x_loaded, 16)
            load_rows(sp, w1_in, w_s1, w_loaded["w1"])
            load_rows(sp, wr_in, w_r, w_loaded["w1"])
            load_rows(sp, wg_in, w_g, w_loaded["g"])
            sp.dma_start(w2_in, w_s2.rearrange("(k p) f -> p k f", p=P)).then_inc(w_loaded["w2"], 16)
            load_quad(1, 1)
            load_quad(0, 0)

            def load_tok(t):
                sp.wait_ge(stats_ready, SB * t)
                sp.dma_start(x_tok[:, :, :], x_v[:, bass.ts(t, SB), :]).then_inc(x_loaded, 16)

            def store(t):
                sp.wait_ge(y_ready, K * t + K)
                for q in range(NQ):
                    sp.dma_start(out_quad[q, :, bass.ts(t, G), :],
                                 y[q * Q:(q + 1) * Q, :, :]).then_inc(y_stored, 16)

            with sp.Fori(0, NT // 2 - 1) as i:
                for parity in range(2):
                    load_tok(2 * i + parity + 2)
                    store(2 * i + parity)
                    load_quad(2 * i + parity + 2, parity)
            store(NT - 2)
            store(NT - 1)
            sp.wait_ge(flag_ready, 1)
            routed = sp.value_load(flag[0:1, 0:1])
            sp.wait_ge(y_stored, 16 * NQ * NT)
            with sp.If(routed > 0):
                with sp.Fori(0, NT) as t:
                    sp.wait_ge(y_stored, t * 16 + 16 * NQ * NT)
                    sp.dma_start(x_tok[:, :, :], x_v[:, bass.ts(t, SB), :]).then_inc(fb_loaded, 16)
                    sp.dma_start(fb_y, out_v[:, bass.ts(t, SB), :]).then_inc(fb_loaded, 16)
                    with sp.Fori(0, NE) as e:
                        sp.wait_ge(fb_y_done, (t * NE + e) * SB + 1)
                        sp.dma_start(fb_w1, w_e1[bass.ds(e, 1), :, :].rearrange("a (k p) f -> p (a k) f", p=P)).then_inc(fb_w_loaded, 16)
                        sp.dma_start(fb_w2, w_e2[bass.ds(e, 1), :, :].rearrange("a (k p) f -> p (a k) f", p=P)).then_inc(fb_w_loaded, 16)
                    sp.wait_ge(fb_y_added, (t + 1) * (NE * SB) + 1)
                    sp.dma_start(out_v[:, bass.ts(t, SB), :], fb_y).then_inc(y_stored, 16)
                sp.wait_ge(y_stored, 16 * NQ * NT + 16 * NT)

        @block.gpsimd
        def _(pool):
            pool.memset(ident[:, :], 0.0).then_inc(ident_zeroed, 1)
            pool.memset(minus_half[:, :], -0.5).then_inc(const_ready, 1)
            pool.memset(ones[:, :], 1.0).then_inc(const_ready, 1)
            pool.wait_ge(ident_zeroed, 1)
            pool.affine_select(out=ident[:, :], in_=ident[:, :], compare_op=ALU.not_equal, fill=1.0,
                               base=0, pattern=[[-1, P]], channel_multiplier=1).then_inc(ident_ready, 1)

            for col, b, row in ((0, b_zf, 0), (0, b_zs, P // 2), (K, b_hf, 0), (K, b_hs, P // 2), (2 * K, b_g, 0)):
                pool.dma_start(bias[row:row + b.shape[0] // K, col:col + K],
                              b.rearrange("(p m) -> p m", m=K)).then_inc(bias_loaded, 16)

            def inverse_std(t):
                pool.wait_ge(var_eps_ready, t + SB)
                pool.tensor_tensor(mean_rstd[:, :, 1], var_eps[:, :], minus_half[:, :], ALU.pow).then_inc(rstd_ready, 1)

            def split_lo(n, lo, full, hi):
                pool.wait_ge(w_hi[n], 1)
                pool.tensor_tensor(lo, full, hi.bitcast(F32), ALU.subtract).then_inc(w_ready[n], 1)

            pool.wait_ge(const_ready, 2)
            for s in range(SB):
                pool.wait_ge(var_eps_ready, s + 1)
                pool.tensor_tensor(mean_rstd[:, s, 1:2], var_eps[:, s:s + 1], minus_half[:, s:s + 1],
                                   ALU.pow).then_inc(rstd_ready, 1)
            split_lo("zf", *half(wz_lo, wz_in, 0), half(wz_hi, wz_in, 0)[0])
            split_lo("hf", *half(wh_lo, wh_in, 0), half(wh_hi, wh_in, 0)[0])
            inverse_std(1)
            pool.wait_ge(w_hi["w1"], 1)
            pool.tensor_tensor(w1_lo[:, :, F:F + NE], wr_in[:, :, :], w1_hi[:, :, F:F + NE].bitcast(F32),
                               ALU.subtract).then_inc(w_ready["w1"], 1)
            split_lo("w1", w1_lo[:, :, 0:F], w1_in[:, :, :], w1_hi[:, :, 0:F])
            split_lo("g", in_order(wg_lo), loaded(wg_in), in_order(wg_hi))
            split_lo("w2", in_order(w2_lo), loaded(w2_in), in_order(w2_hi))
            with pool.Fori(2, NT) as t:
                inverse_std(t)

        @block.scalar
        def _(act):
            act.preload_act_table(ACT.Sigmoid)
            def split_hi(n, hi, full, loads=1):
                act.wait_ge(w_loaded[n], 16 * loads)
                act.activation(hi, full, ACT.Copy).then_inc(w_hi[n], 1)

            def xT_hi_part(t, k):
                act.wait_ge(xT_ready, K * t + k + 1)
                reached(act, products_done, PU * t - PU + FFN1_DONE)
                act.activation(xT_hi[:, k, :], xT_turned(t, k), ACT.Copy).then_inc(xT_hi_ready, 1)

            def turned_hi_part(t, f):
                act.wait_ge(turned, KF * t + f + 1)
                act.activation(hidT_hi[:, f, :], tp[f][:, :], ACT.Copy).then_inc(turned_hi, 1)

            split_hi("zf", *half(wz_hi, wz_in, 0))
            split_hi("zs", *half(wz_hi, wz_in, 1))
            xT_hi_part(0, 0)
            xT_hi_part(0, 1)
            split_hi("hf", *half(wh_hi, wh_in, 0))
            xT_hi_part(0, 2)
            xT_hi_part(0, 3)
            split_hi("hs", *half(wh_hi, wh_in, 1))

            def one_tile(t, parity, last=False):
                for c in range(K):
                    act.wait_ge(products_done, PU * t + 2 * c + 1)
                    reached(act, scan_done, K * t + c - 1)
                    if isinstance(t, int) and t == 0 and c == 0:
                        act.wait_ge(neg_bz_ready, 1)
                    u = pj_bank(Z_H + 2 * c)
                    act.activation(z[:, c % 2, :], u[:, :], ACT.Sigmoid, bias=bias[:, c:c + 1]).then_inc(z_a_ready, 1)
                    act.activation(a[:, c % 2, :], u[:, :], ACT.Sigmoid, bias=neg_bz[:, c:c + 1], scale=-1.0).then_inc(z_a_ready, 1)
                    if c:
                        hi_part(t, c - 1)
                    if isinstance(t, int) and t == 0 and c == 0:
                        act.wait_ge(w_loaded["w1"], 16 * 2)
                        act.activation(w1_hi[:, :, F:F + NE], wr_in[:, :, :], ACT.Copy)
                        split_hi("w1", w1_hi[:, :, 0:F], w1_in[:, :, :], loads=2)
                    if isinstance(t, int) and t == 0 and c == 1:
                        split_hi("g", in_order(wg_hi), loaded(wg_in))
                    if isinstance(t, int) and t == 0 and c == 2:
                        split_hi("w2", in_order(w2_hi), loaded(w2_in))
                    if c == 1 and not last:
                        spread(act, lambda out_, in_: act.activation(out_, in_, ACT.Copy), t + 1)
                for s in range(SB):
                    act.wait_ge(products_done, PU * t + FFN1 + s + 1)
                    reached(act, hid_ready, SB * t + s - 1)
                    act.activation(relu[:, s % 2, :], pj_bank(FFN1 + s)[:, 0:F], ACT.Relu).then_inc(relu_ready, 1)
                    if s == 1:
                        hi_part(t, K - 1)
                for m in range(K):
                    act.wait_ge(products_done, PU * t + GATE[m] + 1)
                    if m == 0:
                        reached(act, y_turned, K * t)
                    act.activation(gate[:, m, :], pj_bank(GATE[m])[:, :], ACT.Sigmoid,
                                   bias=bias[:, 2 * K + m:2 * K + m + 1]).then_inc(gate_ready, 1)
                    if m == 0:
                        for f in range(KF):
                            turned_hi_part(t, f)
                    if not last:
                        xT_hi_part(t + 1, m)

            def hi_part(t, c):
                act.wait_ge(scan_done, K * t + c + 1)
                act.activation(h_hi[:, c, :], h[:, c, :], ACT.Copy).then_inc(h_hi_ready, 1)

            tiles(act, one_tile)
            act.wait_ge(gap_ready, 1)
            act.activation(expo[:, :], gap[:, :], ACT.Exp).then_inc(expo_ready, 1)

        @block.vector
        def _(dve):
            def ln_stats(t):
                reached(dve, x_loaded, 16 * t)
                reached(dve, mean_var_ready, SB * t)
                for s in range(SB):
                    dve.bn_stats(stats[:, s, :], x_tok[:, s, :]).then_inc(stats_ready, 1)

            def ln_stats_done(t):
                dve.wait_ge(stats_ready, SB * t + SB)
                reached(dve, ln_kept, t)
                reached(dve, spread_ready, NQ * NQ * (t - 1))

            def ln_mean_var(t):
                for s in range(SB):
                    dve.bn_aggr(mean_rstd[:, s, :], stats[:, s, :]).then_inc(mean_var_ready, 1)
                dve.wait_ge(mean_var_ready, SB * t + SB)
                dve.tensor_scalar(var_eps[:, :], mean_rstd[:, :, 1], EPS, None, ALU.add).then_inc(var_eps_ready, 1)

            def keep_mean_rstd(t):
                dve.tensor_copy(mean_rstd_all[:, bass.ts(t, SB), :], mean_rstd[:, :, :]).then_inc(ln_kept, 1)

            def ln_apply(t, parity, groups):
                dve.wait_ge(xq_loaded[parity], 8 * NQ * (t - parity) + 16 * NQ)
                dve.wait_ge(spread_ready, NQ * NQ * t)
                reached(dve, xT_ready, K * t)
                if groups[0] == 0:
                    keep_mean_rstd(t)
                for g in groups:
                    dve.tensor_scalar(xn[:, g, :], x_q[:, parity, g, :], mean_rstd_q[:, g, 0:1],
                                      mean_rstd_q[:, g, 1:2], ALU.subtract, ALU.mult).then_inc(xn_ready, 1)

            def turn_x(t, j):
                dve.wait_ge(xn_ready, G * t + G)
                reached(dve, xT_lo_ready, K * t - K + j + 1)
                dve.transpose(xT[:, j, :].rearrange("p (g r) -> p g r", r=Q),
                              xn[:, :, j::K]).then_inc(xT_ready, 1)

            def xT_lo_part(t, k):
                dve.wait_ge(xT_hi_ready, K * t + k + 1)
                dve.tensor_tensor(xT_lo[:, k, :], xT_turned(t, k), xT_hi[:, k, :].bitcast(F32),
                                  ALU.subtract).then_inc(xT_lo_ready, 1)

            def turned_lo_part(t, f):
                dve.wait_ge(turned_hi, KF * t + f + 1)
                dve.tensor_tensor(hidT_lo[:, f, :], tp[f][:, :], hidT_hi[:, f, :].bitcast(F32),
                                  ALU.subtract).then_inc(turned_lo, 1)

            def lo_part(t, c):
                dve.wait_ge(h_hi_ready, K * t + c + 1)
                dve.tensor_tensor(h_lo[:, c, :], h[:, c, :], h_hi[:, c, :].bitcast(F32),
                                  ALU.subtract).then_inc(h_lo_ready, 1)

            def one_tile(t, parity, last=False):
                first = isinstance(t, int) and t == 0
                for c in range(K):
                    dve.wait_ge(z_a_ready, 2 * (K * t + c) + 1)
                    dve.wait_ge(products_done, PU * t + 2 * c + 2)
                    reached(dve, scan_done, K * t + c - 1)
                    dve.scalar_tensor_tensor(zh[:, c % 2, :], pj_bank(Z_H + 2 * c + 1)[:, :], bias[:, K + c:K + c + 1],
                                             z[:, c % 2, :], ALU.add, ALU.mult).then_inc(zh_ready, 1)
                    if c:
                        lo_part(t, c - 1)
                    elif not last:
                        ln_stats(t + 1)
                    dve.wait_ge(z_a_ready, 2 * (K * t + c) + 2)
                    dve.wait_ge(zh_ready, K * t + c + 1)
                    reached(dve, gated_ready, K * t)
                    if c == 0 and not last:
                        ln_stats_done(t + 1)
                    dve.tensor_tensor_scan(h[:, c, :], a[:, c % 2, :], zh[:, c % 2, :],
                                           0.0 if first else h[:, c, TOK - 1:TOK],
                                           ALU.mult, ALU.add).then_inc(scan_done, 1)
                    if not last:
                        if c == 0:
                            ln_mean_var(t + 1)
                        if c >= 2:
                            ln_apply(t + 1, 1 - parity, range((c - 2) * G // 2, (c - 1) * G // 2))
                for s in range(SB):
                    bank = pj_bank(FFN1 + s)
                    dve.wait_ge(relu_ready, SB * t + s + 1)
                    if s == 0:
                        reached(dve, top2_kept, t)
                    dve.tensor_copy(logits[:, bass.ds(t * SB + s, 1), :], bank[:, F:F + NE].rearrange("p (a e) -> p a e", a=1))
                    dve.max(top8[:, s, :], bank[:, F:F + NE]).then_inc(top8_ready, 1)
                    dve.tensor_tensor(hid[:, s, :], bank[:, 0:F], relu[:, s % 2, :], ALU.mult).then_inc(hid_ready, 1)
                    if s == 1:
                        lo_part(t, K - 1)
                dve.wait_ge(top8_ready, SB * t + SB)
                dve.tensor_copy(top2[:, bass.ts(t, SB), :], top8[:, :, 0:2]).then_inc(top2_kept, 1)
                if last:
                    dve.wait_ge(top2_kept, NT)
                    dve.tensor_tensor(gap[:, :], top2[:, :, 1], top2[:, :, 0], ALU.subtract).then_inc(gap_ready, 1)
                def gated(m):
                    dve.wait_ge(gate_ready, K * t + m + 1)
                    dve.tensor_tensor(gate[:, m, :], gate[:, m, :], h[:, m, :], ALU.mult).then_inc(gated_ready, 1)

                def plus_ffn(m):
                    dve.wait_ge(products_done, PU * t + OUT[m] + 1)
                    dve.wait_ge(gated_ready, K * t + m + 1)
                    dve.tensor_tensor(gate[:, m, :], pj_bank(OUT[m])[:, :], gate[:, m, :], ALU.add).then_inc(sum_ready, 1)

                def turn_y(m):
                    if m == 0:
                        reached(dve, y_stored, 16 * NQ * t)
                    dve.wait_ge(sum_ready, K * t + m + 1)
                    dve.transpose(y[:, :, m::K], gate[:, m, :].rearrange("p (g r) -> p g r", r=Q)).then_inc(y_turned, 1)

                def plus_x(m):
                    if first and m == 0:
                        dve.wait_ge(xq_loaded[0], 16 * NQ)
                    dve.wait_ge(y_turned, K * t + m + 1)
                    dve.tensor_tensor(y[:, :, m::K], y[:, :, m::K], x_q[:, parity, :, m::K], ALU.add).then_inc(y_ready, 1)

                def next_x(turns, split):
                    if not last:
                        for j in turns:
                            turn_x(t + 1, j)
                        for k in split:
                            xT_lo_part(t + 1, k)

                next_x((0, 1), ())
                for f in range(KF):
                    turned_lo_part(t, f)
                gated(0)
                next_x((2,), (0,))
                gated(1)
                next_x((3,), (1,))
                plus_ffn(0)
                gated(2)
                next_x((), (2,))
                turn_y(0)
                plus_ffn(1)
                turn_y(1)
                plus_x(0)
                plus_x(1)
                gated(3)
                next_x((), (3,))
                plus_ffn(2)
                turn_y(2)
                plus_ffn(3)
                plus_x(2)
                turn_y(3)
                plus_x(3)

            def split_lo(n, lo, full, hi):
                dve.wait_ge(w_hi[n], 1)
                dve.tensor_tensor(lo, full, hi.bitcast(F32), ALU.subtract).then_inc(w_ready[n], 1)

            for s in range(SB):
                dve.wait_ge(x0_loaded[s], 16)
                dve.bn_stats(stats[:, s, :], x_tok[:, s, :]).then_inc(stats_ready, 1)
                dve.wait_ge(stats_ready, s + 1)
                dve.bn_aggr(mean_rstd[:, s, :], stats[:, s, :]).then_inc(mean_var_ready, 1)
                dve.wait_ge(mean_var_ready, s + 1)
                dve.tensor_scalar(var_eps[:, s:s + 1], mean_rstd[:, s, 1:2], EPS, None, ALU.add).then_inc(var_eps_ready, 1)
            for s in range(SB):
                dve.wait_ge(rstd_ready, s + 1)
                dve.tensor_scalar(xn_tok[:, s, :], x_tok[:, s, :], mean_rstd[:, s, 0:1], mean_rstd[:, s, 1:2],
                                  ALU.subtract, ALU.mult).then_inc(xn_ready, G // SB)
            keep_mean_rstd(0)
            split_lo("zs", *half(wz_lo, wz_in, 1), half(wz_hi, wz_in, 1)[0])
            for k in range(K):
                xT_lo_part(0, k)
            split_lo("hs", *half(wh_lo, wh_in, 1), half(wh_hi, wh_in, 1)[0])
            dve.wait_ge(bias_loaded, 16 * 5)
            dve.tensor_scalar(neg_bz[:, :], bias[:, 0:K], -1.0, None, ALU.mult).then_inc(neg_bz_ready, 1)
            tiles(dve, one_tile)

            dve.wait_ge(expo_ready, 1)
            dve.tensor_scalar(denom[:, :], expo[:, :], 1.0, None, ALU.add).then_inc(route_step, 1)
            dve.wait_ge(route_step, 1)
            dve.tensor_scalar(is_one[:, :], denom[:, :], 1.0, None, ALU.is_le).then_inc(route_step, 1)
            dve.wait_ge(route_step, 2)
            dve.tensor_reduce(n_ones[:, :], is_one[:, :], AX_X, ALU.add).then_inc(route_step, 1)
            dve.wait_ge(counted, 1)
            dve.tensor_copy(flag[:, :], tp[0][0:1, 0:1]).then_inc(flag_ready, 1)

            dve.wait_ge(flag_ready, 1)
            routed = dve.value_load(flag[0:1, 0:1])
            with dve.If(routed > 0):
                top1 = top2[:, :, 0:1].to_broadcast([P, NB, NE])
                dve.tensor_tensor(prob, logits[:, :, :], top1, ALU.is_equal).then_inc(fb_route, 1)
                dve.wait_ge(fb_route, 1)
                ones_b = is_one[:, :].rearrange("p (b a) -> p b a", a=1).to_broadcast([P, NB, NE])
                dve.tensor_tensor(prob, prob, ones_b, ALU.mult).then_inc(fb_route, 1)
                dve.wait_ge(fb_route, 2)
                prob_flat = xT[:, 0, :]
                mean_rstd_flat = mean_rstd_all[:, :, :].rearrange("p b v -> p (b v)")
                dve.sem_inc(fb_y_added, 1)
                with dve.Fori(0, NT) as t:
                    dve.wait_ge(fb_loaded, (t + 1) * 32)
                    for s in range(SB):
                        dve.tensor_scalar(xn_tok[:, s, :], x_tok[:, s, :], mean_rstd_flat[:, bass.ds(t * (2 * SB) + 2 * s, 1)],
                                          mean_rstd_flat[:, bass.ds(t * (2 * SB) + 2 * s + 1, 1)],
                                          ALU.subtract, ALU.mult).then_inc(fb_xn_ready, 1)
                    for k in range(K):
                        dve.wait_ge(fb_turned, t * K + k + 1)
                        dve.tensor_copy(fb_xT[:, k, :], pj[k][:, :]).then_inc(fb_xT_ready, 1)
                    with dve.Fori(0, NE) as e:
                        for s in range(SB):
                            dve.wait_ge(fb_hid_done, (t * NE + e) * SB + s + 1)
                            dve.tensor_scalar(relu[:, 0, :], pj[s][:, 0:F], 0.0, None, ALU.max).then_inc(fb_relu, 1)
                            dve.wait_ge(fb_relu, (t * NE + e) * SB + s + 1)
                            dve.scalar_tensor_tensor(hid[:, s, :], pj[s][:, 0:F],
                                                     prob_flat[:, bass.ds(t * (SB * NE) + s * NE + e, 1)],
                                                     relu[:, 0, :], ALU.mult, ALU.mult).then_inc(fb_hid_ready, 1)
                            dve.wait_ge(fb_hid_ready, (t * NE + e) * SB + s + 1)
                        for f in range(KF):
                            dve.wait_ge(fb_hid_turned, (t * NE + e) * KF + f + 1)
                            dve.tensor_copy(fb_hidT[:, f, :], tp[f][:, :]).then_inc(fb_hidT_ready, 1)
                        for s in range(SB):
                            dve.wait_ge(fb_y_done, (t * NE + e) * SB + s + 2)
                            dve.tensor_tensor(fb_y[:, s, :], pj[s][:, :], fb_y[:, s, :], ALU.add).then_inc(fb_y_added, 1)
                        dve.wait_ge(fb_y_added, (t * NE + e + 1) * SB + 1)

        @block.tensor
        def _(pe):
            def three(dst, pairs, hook=None):
                for i, (s_hi, s_lo, m_hi, m_lo) in enumerate(pairs):
                    if hook:
                        hook(i)
                    for j, (st, mv) in enumerate(((s_hi, m_hi), (s_lo, m_hi), (s_hi, m_lo))):
                        end = i == len(pairs) - 1 and j == 2
                        mm = pe.matmul(dst, st, mv, start=(i == 0 and j == 0), stop=end)
                return mm

            def keep_busy(n):
                for _ in range(n):
                    pe.transpose(tp[0][:, 0:P], ident[:, :], ident[:, :])

            def turn(bank, sources):
                for s, src in enumerate(sources):
                    mm = pe.transpose(bank[:, s * P:(s + 1) * P], src, ident[:, :])
                mm.then_inc(turned, 1)

            def turn_hid(t, f):
                if f == 0:
                    pe.wait_ge(hid_ready, SB * t + SB)
                reached(pe, turned_lo, KF * t - KF + f + 1)
                turn(tp[f], [hid[:, s, f * P:(f + 1) * P] for s in range(SB)])

            def columns(w, k, m):
                return w[:, k, m * P:(m + 1) * P]

            def one_tile(t, parity, last=False):
                first = isinstance(t, int) and t == 0

                for c in range(K):
                    for kind, (whi, wlo) in enumerate(((wz_hi, wz_lo), (wh_hi, wh_lo))):
                        u = 2 * c + kind
                        if u in (0, 2):
                            reached(pe, gate_ready, K * t - 1 + u // 2)
                        elif u < NPJ:
                            reached(pe, sum_ready, K * t - {1: 2, 3: 1, 4: 0}[u])
                        elif u % 2 == 1:
                            pe.wait_ge(z_a_ready, 2 * (K * t + (u - NPJ) // 2) + 2)
                        else:
                            pe.wait_ge(zh_ready, K * t + (u - NPJ) // 2 + 1)
                        if first:
                            for half in "fs":
                                pe.wait_ge(w_ready["zh"[kind] + half], 1)
                        three(pj_bank(u)[:, :],
                              [(columns(whi, k, c), columns(wlo, k, c), xT_hi[:, k, :], xT_lo[:, k, :]) for k in range(K)],
                              (lambda k: pe.wait_ge(xT_lo_ready, K * t + k + 1)) if u == 0 else None,
                              ).then_inc(products_done, 1)
                for s in range(SB):
                    if s % 2:
                        pe.wait_ge(z_a_ready, 2 * (K * t + (3 + s) // 2) + 2)
                    else:
                        pe.wait_ge(zh_ready, K * t + (3 + s) // 2 + 1)
                    if first:
                        pe.wait_ge(w_ready["w1"], 2)
                    tok = slice(s * P, (s + 1) * P)
                    three(pj_bank(FFN1 + s)[:, 0:F + NE],
                          [(xT_hi[:, k, tok], xT_lo[:, k, tok], w1_hi[:, k, :], w1_lo[:, k, :]) for k in range(K)],
                          ).then_inc(products_done, 1)
                def gate_product(m):
                    if first and m == 0:
                        pe.wait_ge(w_ready["g"], 1)
                    three(pj_bank(GATE[m])[:, :],
                          [(columns(wg_hi, k, m), columns(wg_lo, k, m), h_hi[:, k, :], h_lo[:, k, :]) for k in range(K)],
                          (lambda k: pe.wait_ge(h_lo_ready, K * t + k + 1)) if m == 0 else None,
                          ).then_inc(products_done, 1)

                def out_product(m):
                    if first and m == 0:
                        pe.wait_ge(w_ready["w2"], 1)
                    three(pj_bank(OUT[m])[:, :],
                          [(columns(w2_hi, f, m), columns(w2_lo, f, m), hidT_hi[:, f, :], hidT_lo[:, f, :]) for f in range(KF)],
                          ).then_inc(products_done, 1)

                pe.wait_ge(zh_ready, K * t + K)
                gate_product(0)
                for f in range(KF):
                    turn_hid(t, f)
                pe.wait_ge(hid_ready, SB * t + 1)
                gate_product(1)
                pe.wait_ge(hid_ready, SB * t + 2)
                pe.wait_ge(turned_lo, KF * t + KF)
                out_product(0)
                pe.wait_ge(hid_ready, SB * t + 3)
                gate_product(2)
                pe.wait_ge(hid_ready, SB * t + 4)
                out_product(1)
                pe.wait_ge(gate_ready, K * t + 1)
                gate_product(3)
                pe.wait_ge(gate_ready, K * t + 2)
                out_product(2)
                pe.wait_ge(sum_ready, K * t + 1)
                out_product(3)

            pe.wait_ge(ident_ready, 1)
            keep_busy(36)
            for s in range(SB):
                pe.wait_ge(xn_ready, (s + 1) * G // SB)
                for j in range(K):
                    mm = pe.transpose(pj[j + 1][:, s * P:(s + 1) * P], xn_tok[:, s, j::K], ident[:, :])
                    if s == SB - 1:
                        mm.then_inc(xT_ready, 1)
            keep_busy(10)
            tiles(pe, one_tile)
            pe.wait_ge(route_step, 3)
            pe.wait_ge(const_ready, 2)
            pe.matmul(tp[0][0:1, 0:1], n_ones[:, :], ones[:, :], start=True, stop=True).then_inc(counted, 1)

            pe.wait_ge(flag_ready, 1)
            routed = pe.value_load(flag[0:1, 0:1])
            with pe.If(routed > 0):
                pe.wait_ge(sum_ready, K * NT)
                pe.sem_inc(fb_y_done, 1)
                with pe.Fori(0, NT) as t:
                    pe.wait_ge(fb_xn_ready, (t + 1) * SB)
                    for k in range(K):
                        for s in range(SB):
                            mm = pe.transpose(pj[k][:, s * P:(s + 1) * P], xn_tok[:, s, k * P:(k + 1) * P], ident[:, :])
                        mm.then_inc(fb_turned, 1)
                    with pe.Fori(0, NE) as e:
                        pe.wait_ge(fb_xT_ready, (t + 1) * K)
                        pe.wait_ge(fb_y_added, (t * NE + e) * SB + 1)
                        pe.wait_ge(fb_w_loaded, (t * NE + e + 1) * 32)
                        for s in range(SB):
                            for k in range(K):
                                mm = pe.matmul(pj[s][:, 0:F], fb_xT[:, k, s * P:(s + 1) * P], fb_w1[:, k, :],
                                               start=(k == 0), stop=(k == K - 1))
                            mm.then_inc(fb_hid_done, 1)
                        pe.wait_ge(fb_hid_ready, (t * NE + e + 1) * SB)
                        for f in range(KF):
                            for s in range(SB):
                                mm = pe.transpose(tp[f][:, s * P:(s + 1) * P], hid[:, s, f * P:(f + 1) * P], ident[:, :])
                            mm.then_inc(fb_hid_turned, 1)
                        pe.wait_ge(fb_hidT_ready, (t * NE + e + 1) * KF)
                        for s in range(SB):
                            for f in range(KF):
                                mm = pe.matmul(pj[s][:, :], fb_hidT[:, f, s * P:(s + 1) * P], fb_w2[:, f, :],
                                               start=(f == 0), stop=(f == KF - 1))
                            mm.then_inc(fb_y_done, 1)


_INS = ['L0_attn_x', 'L0_attn_W_zf', 'L0_attn_b_zf', 'L0_attn_W_hf', 'L0_attn_b_hf', 'L0_attn_W_zs', 'L0_attn_b_zs',
        'L0_attn_W_hs', 'L0_attn_b_hs', 'L0_attn_W_g', 'L0_attn_b_g', 'L0_ffn_Ws1', 'L0_ffn_Ws2', 'L0_ffn_W1',
        'L0_ffn_W2', 'L0_ffn_Wr']
_OUTS = [((1, 8192, 512), 'float32')]


def kernel(**inputs):
    import numpy as _np
    import concourse.bacc as _bacc
    from concourse import mybir as _mybir
    from concourse.bass_utils import run_bass_kernel_spmd as _run

    nc = _bacc.Bacc("TRN2", target_bir_lowering=False, num_devices=1)
    arrays, args = {}, []
    for name in _INS:
        a = _np.ascontiguousarray(inputs[name])
        arrays[f"in_{name}_dram"] = a
        args.append(nc.dram_tensor(f"in_{name}_dram", a.shape, _mybir.dt.from_np(a.dtype), kind="ExternalInput").ap())
    for i, (shape, dtype) in enumerate(_OUTS):
        dt = _mybir.dt.from_np(_np.dtype(dtype))
        args.append(nc.dram_tensor(f"out_{i}_dram", shape, dt, kind="ExternalOutput").ap())
    minlstm_gated_moe_kernel(nc, *args)
    r = _run(nc, [arrays], core_ids=[0])
    got = tuple(r.results[0][f"out_{i}_dram"] for i in range(len(_OUTS)))
    return got[0]
```
